# Optimizing a Trainium2 kernel written in Bass

```python
import numpy as np
import jax
import jax.numpy as jnp

def _softmax(x, axis=-1):
    return jax.nn.softmax(x, axis=axis)

def _gelu(x):
    return jax.nn.gelu(x, approximate=True)

def _silu(x):
    return jax.nn.silu(x)

def _sigmoid(x):
    return jax.nn.sigmoid(x)

def _layernorm(x, axis=-1, eps=1e-05):
    m = jnp.mean(x, axis=axis, keepdims=True)
    v = jnp.var(x, axis=axis, keepdims=True)
    return (x - m) / jnp.sqrt(v + eps)

def _scatter_add(tgt, idx, src, axis=0):
    return tgt.at[idx].add(src)

def _segment_sum(src, seg, n):
    return jax.ops.segment_sum(src, seg, n)
kernel_name = 'mk_adj_ffn_d1_adj_r2_d4e1c9'

def setup_inputs(seed: int=0):
    np.random.seed(seed)
    _w = jnp.asarray

    def _rec_inputs():
        import jax
        import jax.numpy as jnp
        _gk = jax.random.key(seed)
        x = -0.0005207 + 1.001 * jax.random.normal(jax.random.fold_in(_gk, 1), (32, 256, 128), jnp.float32)
        _a = jax.random.bernoulli(jax.random.fold_in(_gk, 2), 0.0625, (256, 256))
        _a = jnp.logical_or(_a, jnp.swapaxes(_a, -1, -2))
        _a = jnp.logical_or(_a, jnp.eye(256, dtype=bool))
        adj = _a.astype(jnp.int32)
        return (x, adj)
    x, adj = _rec_inputs()

    def _L0_gnn_setup():
        import jax, jax.numpy as jnp
        import numpy as np
        ALPHA = 0.2
        MASK_VAL = -9000000000000000.0
        key = jax.random.key(seed)
        k1, k2, k3, k4 = jax.random.split(key, 4)
        B, N, F = (8, 512, 128)
        H, OUT = (4, 128)
        hs = OUT // H
        x = jax.random.normal(k1, (B, N, F), dtype=jnp.float32)
        adj = jax.random.randint(k2, (N, N), 0, 2, dtype=jnp.int32)
        wb = float(np.sqrt(6.0 / (F + hs)))
        ab = float(np.sqrt(6.0 / (H + 2 * hs)))
        W = jax.random.uniform(k3, (H, F, hs), dtype=jnp.float32, minval=-wb, maxval=wb)
        a = jax.random.uniform(k4, (H, 2 * hs), dtype=jnp.float32, minval=-ab, maxval=ab)
        return {'x': x, 'adj': adj, 'W': W, 'a': a}
    _L0_gnn_all = _L0_gnn_setup()
    _L0_gnn_in = {k: v for k, v in _L0_gnn_all.items() if k in ('W', 'a')}
    del _L0_gnn_all

    def _L0_ffn_setup():
        import jax, jax.numpy as jnp
        import numpy as np
        C = 128
        HID = 512
        E = 8
        TEMP = 1.0
        key = jax.random.key(seed)
        ks = jax.random.split(key, 7)
        x = jax.random.normal(ks[0], (8, 8192, C), dtype=jnp.float32)
        W1 = jax.random.normal(ks[1], (C, HID), dtype=jnp.float32) * 0.02
        b1 = jnp.zeros((HID,), dtype=jnp.float32)
        Wg = jax.random.normal(ks[2], (HID, E), dtype=jnp.float32) * 0.02
        bg = jnp.zeros((E,), dtype=jnp.float32)
        Wd = jax.random.normal(ks[3], (E, HID, C), dtype=jnp.float32) * 0.02
        bd = jnp.zeros((E, C), dtype=jnp.float32)
        return {'x': x, 'W1': W1, 'b1': b1, 'Wg': Wg, 'bg': bg, 'Wd': Wd, 'bd': bd}
    _L0_ffn_all = _L0_ffn_setup()
    _L0_ffn_in = {k: v for k, v in _L0_ffn_all.items() if k in ('W1', 'b1', 'Wg', 'bg', 'Wd', 'bd')}
    del _L0_ffn_all
    return {'x': x, 'adj': adj, 'L0_gnn_W': _L0_gnn_in['W'], 'L0_gnn_a': _L0_gnn_in['a'], 'L0_ffn_W1': _L0_ffn_in['W1'], 'L0_ffn_b1': _L0_ffn_in['b1'], 'L0_ffn_Wg': _L0_ffn_in['Wg'], 'L0_ffn_bg': _L0_ffn_in['bg'], 'L0_ffn_Wd': _L0_ffn_in['Wd'], 'L0_ffn_bd': _L0_ffn_in['bd']}

def reference(x, adj, L0_gnn_W, L0_gnn_a, L0_ffn_W1, L0_ffn_b1, L0_ffn_Wg, L0_ffn_bg, L0_ffn_Wd, L0_ffn_bd):
    import jax
    import jax.numpy as jnp

    def _L0_gnn_ref(x, adj, W, a):
        import jax, jax.numpy as jnp
        import numpy as np
        ALPHA = 0.2
        MASK_VAL = -9000000000000000.0
        B, N, _ = x.shape
        H, _, hs = W.shape
        Wh = jnp.einsum('bnf,hfd->bhnd', x, W)
        a1, a2 = (a[:, :hs], a[:, hs:])
        ei = jnp.einsum('bhnd,hd->bhn', Wh, a1)
        ej = jnp.einsum('bhnd,hd->bhn', Wh, a2)
        e = ei[:, :, :, None] + ej[:, :, None, :]
        e = jnp.where(e > 0, e, ALPHA * e)
        e = jnp.where(adj[None, None] > 0, e, MASK_VAL)
        att = jax.nn.softmax(e, axis=-1)
        h = jnp.einsum('bhij,bhjd->bhid', att, Wh)
        h = h.transpose(0, 2, 1, 3).reshape(B, N, H * hs)
        return jax.nn.elu(h)

    def _L0_ffn_ref(x, W1, b1, Wg, bg, Wd, bd):
        import jax, jax.numpy as jnp
        import numpy as np
        C = 128
        HID = 512
        E = 8
        TEMP = 1.0
        orig_shape = x.shape
        xf = x.reshape(-1, orig_shape[-1])
        H = jax.nn.gelu(xf @ W1 + b1, approximate=False)
        probs = jax.nn.softmax((H @ Wg + bg) / TEMP, axis=-1)
        assign = jnp.argmax(probs, axis=-1)
        out = jnp.zeros_like(xf)
        for e in range(Wd.shape[0]):
            y = H @ Wd[e] + bd[e]
            sel = (assign == e)[:, None]
            out = out + jnp.where(sel, probs[:, e:e + 1] * y, 0.0)
        return out.reshape(orig_shape)
    x = x + _L0_gnn_ref(_layernorm(x, axis=-1), adj, L0_gnn_W, L0_gnn_a)
    x = x + _L0_ffn_ref(_layernorm(x, axis=-1), L0_ffn_W1, L0_ffn_b1, L0_ffn_Wg, L0_ffn_bg, L0_ffn_Wd, L0_ffn_bd)
    return x

_drawn_inputs = setup_inputs


def setup_inputs(seed=0):
    import zlib

    import numpy as np

    out = dict(_drawn_inputs(seed))
    spreads = {'L0_ffn_b1': (0.0, 0.8), 'L0_ffn_bg': (0.0, 0.471), 'L0_ffn_bd': (0.0, 0.611)}
    factors = {'L0_ffn_W1': 5.467, 'L0_ffn_Wg': 5.383, 'L0_ffn_Wd': 6.994}
    for name, (base, spread) in spreads.items():
        noise = np.random.default_rng([zlib.crc32(name.encode()), seed]).standard_normal(out[name].shape)
        drawn = base * np.exp(spread * noise) if base else spread * noise
        out[name] = jnp.asarray(drawn.astype(out[name].dtype))
    for name, factor in factors.items():
        out[name] = (out[name] * factor).astype(out[name].dtype)
    return out
```

```python
from collections import namedtuple
from contextlib import ExitStack

import concourse.bass as bass
from concourse import mybir

ALU = mybir.AluOpType
ACT = mybir.ActivationFunctionType
AX = mybir.AxisListType
F32 = mybir.dt.float32
F16 = mybir.dt.float16
BF16 = mybir.dt.bfloat16
I32 = mybir.dt.int32
U32 = mybir.dt.uint32
MAX = bass.bass_isa.ReduceOp.max

P = 128
B, N, F = 32, 256, 128
H, D = 4, 32
HID, E = 512, 8
KC = HID // P
TILES = B * N // P
Q = 4
GT = Q * P
GROUPS = TILES // Q
GB = GT // N
JT = N // P
D1 = D + 1
EPS = 1e-5
SCALE_LN = 10 * 0.6931471805599453
START1 = 6
SLOTS = TILES + E
SGROUPS = SLOTS // Q
LIST = B * N + P
NOBODY = B * N
ROW = F + 4
STEEP = 2.0 ** 100
W_SCALE = 2.0 ** 8

Group = namedtuple("Group", "n k p")


def run_stages(eng, groups, buffers, start, stages):
    last = max(lag for lag, _ in stages)

    def peeled(t):
        for lag, body in stages:
            n = t - lag
            if 0 <= n < groups:
                body(Group(n, n // buffers, n % buffers))

    for t in range(start):
        peeled(t)
    with eng.Fori(start // buffers, groups // buffers) as i:
        for u in range(buffers):
            for lag, body in stages:
                body(Group(buffers * i + (u - lag), i + (u - lag) // buffers, (u - lag) % buffers))
    for t in range(groups, groups + last):
        peeled(t)


def from_group(G, first):
    return not isinstance(G.n, int) or G.n >= first


def wait_apart(eng, sem, value, passed):
    eng.wait_ge(sem, value)
    eng.sem_inc(passed, 1)


def build(nc, x, adj, W, a, W1, b1, Wg, bg, Wd, bd, out):
    ctx = ExitStack()
    with ctx:
        def sb(name, shape, dt=F32):
            return ctx.enter_context(nc.sbuf_tensor(name, shape, dt))

        def sem(name):
            return ctx.enter_context(nc.semaphore(name))

        lists = nc.dram_tensor("lists", (E * LIST + P, ROW), F32, kind="Internal").ap()

        x_all = sb("x_all", [P, TILES, F])
        ident = sb("ident", [P, P])
        Wd_sb = sb("Wd_sb", [P, E * KC, F])
        bd_sb = sb("bd_sb", [1, E * F])
        W1_sb = sb("W1_sb", [P, HID])
        b1_sb = sb("b1_sb", [P, KC])
        Wg_sb = sb("Wg_sb", [P, KC, E])
        bg_sb = sb("bg_sb", [P, E])
        ones_row = sb("ones_row", [1, P])
        mhalf = sb("mhalf", [P, Q])
        ones = sb("ones", [P, Q, F])
        W1_hi = sb("W1_hi", [P, HID], F16)
        W1_lo = sb("W1_lo", [P, HID], F16)
        adj_i = sb("adj_i", [P, JT, N], I32)
        adj_f = sb("adj_f", [P, JT, N])
        mask = sb("mask", [P, JT, N], BF16)
        negmask = sb("negmask", [P, JT, N], BF16)
        a_sb = sb("a_sb", [P, H, 2, D])
        wa_prod = sb("wa_prod", [P, 2, H, D])
        Wcat = sb("Wcat", [P, F + 3 * H])
        Wa1rep = sb("Wa1rep", [P, H, P])
        stats = [sb(f"stats{i}", [P, Q, 6]) for i in range(2)]
        mv = [sb(f"mv{i}", [P, Q, 2]) for i in range(2)]
        veps = [sb(f"veps{i}", [P, Q]) for i in range(2)]
        rstd = [sb(f"rstd{i}", [P, Q]) for i in range(2)]
        xn = [sb(f"xn{i}", [P, Q, F]) for i in range(2)]
        xTs = [sb(f"xTs{i}", [P, GT]) for i in range(2)]
        eh = [sb(f"eh{i}", [P, 3, Q, H]) for i in range(2)]
        emax = [sb(f"emax{i}", [P, GB, H]) for i in range(2)]
        guard = [sb(f"guard{i}", [P, GB, H]) for i in range(2)]
        shifted = [sb(f"shifted{i}", [P, 2, Q, H]) for i in range(2)]
        args = [sb(f"args{i}", [P, 3, Q, H]) for i in range(2)]
        ex = [sb(f"ex{i}", [P, 3, Q, H]) for i in range(2)]
        V = [sb(f"V{i}", [P, Q, H, 2, D1]) for i in range(2)]
        Vhi = [sb(f"Vhi{i}", [P, Q, H, 2, D1], F16) for i in range(2)]
        Vlo = [sb(f"Vlo{i}", [P, Q, H, 2, D1], F16) for i in range(2)]
        steep = [sb(f"steep{i}", [P, GB, JT, N], BF16) for i in range(2)]
        C = [sb(f"C{i}", [P, H, GB, JT, N], BF16) for i in range(2)]
        rB = sb("rB", [P, Q, H, D1])
        num = [sb(f"num{i}", [P, Q, H, D1]) for i in range(2)]
        rden = [sb(f"rden{i}", [P, Q, H]) for i in range(2)]
        hh = [sb(f"hh{i}", [P, Q, F]) for i in range(2)]
        eh_exp = [sb(f"eh_exp{i}", [P, Q, F]) for i in range(2)]
        xm1 = [sb(f"xm1{i}", [P, Q, F]) for i in range(2)]
        x_relu = sb("x_relu", [P, Q, F])

        bank = [ctx.enter_context(nc.psum_tensor(f"bank{i}", [P, 512], F32)) for i in range(8)]
        xT_ps = bank[0]
        Wh_ps = [bank[1], bank[2]]
        ei_ps = [bank[3], bank[4]]
        agg_ps = [bank[5], bank[6]]
        setup_ps = bank[7]

        s_w = sem("weights_loaded")
        s_passed = sem("waits_passed")
        s_adj = sem("adj_loaded")
        s_x = [sem("x_loaded0"), sem("x_loaded1")]
        s_const = sem("constants_ready")
        s_adjf = sem("adj_float")
        s_adjT = sem("adj_transposed")
        s_mask = sem("mask_ready")
        s_wa = sem("wa_ready")
        s_bn = sem("stats_of_tiles")
        s_mv = sem("mean_var_ready")
        s_veps = sem("var_eps")
        s_rstd = sem("rstd_ready")
        s_xn = sem("normalised")
        s_xT = sem("transposed")
        s_xTs = sem("transposed_in_sbuf")
        s_wh = sem("wh_ready")
        s_ei = sem("ei_broadcast")
        s_eh = sem("e_in_sbuf")
        s_emax = sem("e_max_of_tiles")
        s_guard = sem("guard_ready")
        s_shift = sem("e_shifted")
        s_clamp = sem("ei_clamped")
        s_args = sem("exp_args_ready")
        s_ex = sem("exps_ready")
        s_V = sem("V_ready")
        s_Vhi = sem("V_high_part")
        s_Vlo = sem("V_low_part")
        s_steep = sem("steep_of_heads")
        s_C = sem("C_of_heads")
        s_agg = sem("sums_of_tiles")
        s_rB = sem("rB_of_tiles")
        s_num = sem("numerators_of_tiles")
        s_rden = sem("denominator_inverted")
        s_hh = sem("h_ready")
        s_eexp = sem("exp_h_ready")
        s_xm1 = sem("x_minus_1")
        s_relu = sem("x_plus_relu")
        s_x2 = sem("x2_ready")

        block1 = nc.Block()
        block = block1.__enter__()

        WLOADS = 9

        @block.sync
        def _(sp):
            sp.dma_start(adj_i[:], adj.rearrange("(t p) j -> p t j", p=P)).then_inc(s_adj, 16)
            with nc.allow_non_contiguous_dma(reason="small weights, once"):
                sp.dma_start(Wcat[:, 0:F].rearrange("p (h d) -> p h d", h=H),
                             W.rearrange("h f d -> f h d")).then_inc(s_w, 16)
                sp.dma_start(a_sb[:].rearrange("p h t d -> p (h t d)"),
                             a.rearrange("h t -> (h t)").partition_broadcast(P)).then_inc(s_w, 16)
                sp.dma_start(b1_sb[:], b1.rearrange("(k p) -> p k", p=P)).then_inc(s_w, 16)
                sp.dma_start(Wg_sb[:], Wg.rearrange("(k p) e -> p k e", p=P)).then_inc(s_w, 16)
                sp.dma_start(bg_sb[:], bg.partition_broadcast(P)).then_inc(s_w, 16)

            def load_x(G):
                if from_group(G, 2):
                    sp.wait_ge(s_mv, G.n - 1)
                sp.dma_start(x_all[:, bass.ds(G.n * Q, Q), 0:F],
                             x[bass.ds(G.n * GT, GT), :].rearrange("(t p) f -> p t f", p=P)
                             ).then_inc(s_x[G.p], 16)

            run_stages(sp, GROUPS, 2, 4, [(0, load_x)])

        @block.gpsimd
        def _(pool):
            pool.memset(ident[:], 1.0).then_inc(s_const, 1)
            pool.memset(ones_row[:], 1.0).then_inc(s_const, 1)
            pool.memset(mhalf[:], -0.5).then_inc(s_const, 1)
            pool.memset(ones[:], 1.0).then_inc(s_const, 1)
            pool.wait_ge(s_const, 1)
            pool.affine_select(out=ident[:], in_=ident[:], compare_op=ALU.is_equal, fill=0.0,
                               base=0, pattern=[[-1, P]], channel_multiplier=1).then_inc(s_const, 1)

            def rstd_of(G):
                wait_apart(pool, s_mv, G.n + 1, s_passed)
                pool.tensor_scalar(veps[G.p][:], mv[G.p][:, :, 1], EPS, None, ALU.add).then_inc(s_veps, 1)
                pool.wait_ge(s_veps, G.n + 1)
                pool.tensor_tensor(rstd[G.p][:], veps[G.p][:], mhalf[:], ALU.pow).then_inc(s_rstd, 1)

            def guard_args(G):
                wait_apart(pool, s_emax, G.n + 1, s_passed)
                pool.partition_all_reduce(guard[G.p][:].rearrange("p b h -> p (b h)"),
                                          emax[G.p][:].rearrange("p b h -> p (b h)"), P, MAX
                                          ).then_inc(s_guard, 1)
                pool.wait_ge(s_guard, G.n + 1)
                for b in range(GB):
                    g_b = guard[G.p][:, b:b + 1, :].broadcast_to([P, JT, H])
                    t_b = slice(b * JT, (b + 1) * JT)
                    pool.tensor_tensor(shifted[G.p][:, 0, t_b, :], eh[G.p][:, 0, t_b, :], g_b, ALU.subtract)
                    last = pool.tensor_tensor(shifted[G.p][:, 1, t_b, :], eh[G.p][:, 1, t_b, :], g_b, ALU.add)
                last.then_inc(s_shift, 1)
                wait_apart(pool, s_shift, G.n + 1, s_passed)
                pool.tensor_scalar(args[G.p][:, 0], shifted[G.p][:, 0], 1.0, SCALE_LN, ALU.mult, ALU.add)
                pool.tensor_scalar(args[G.p][:, 1], shifted[G.p][:, 0], 0.2, SCALE_LN, ALU.mult, ALU.add)
                pool.tensor_scalar(args[G.p][:, 2], shifted[G.p][:, 1], 0.0, -0.8, ALU.max, ALU.mult
                                   ).then_inc(s_args, 1)

            def V_low(G):
                pool.wait_ge(s_V, G.n + 1)
                pool.wait_ge(s_Vhi, G.n + 1)
                flat = "p q h t d -> p (q h t d)"
                pool.tensor_tensor(Vlo[G.p][:].rearrange(flat), V[G.p][:].rearrange(flat),
                                   Vhi[G.p][:].rearrange(flat), ALU.subtract).then_inc(s_Vlo, 1)

            def x_minus_1(G):
                if from_group(G, 2):
                    pool.wait_ge(s_x2, G.n - 1)
                pool.tensor_tensor(xm1[G.p][:], x_all[:, bass.ds(G.n * Q, Q), 0:F], ones[:], ALU.subtract
                                   ).then_inc(s_xm1, 1)

            def h_out(G):
                pool.wait_ge(s_rden, G.n + 1)
                pool.tensor_tensor(hh[G.p][:].rearrange("p q (h d) -> p (q h) d", h=H),
                                   num[G.p][:, :, :, 0:D].rearrange("p q h d -> p (q h) d"),
                                   rden[G.p][:].rearrange("p q h -> p (q h)").unsqueeze(2).broadcast_to([P, Q * H, D]),
                                   ALU.mult).then_inc(s_hh, 1)

            run_stages(pool, GROUPS, 2, START1, [(2, guard_args), (0, rstd_of), (3, x_minus_1), (3, h_out), (2, V_low)])

        @block.scalar
        def _(act):
            act.dma_start(W1_sb[:], W1[:, :]).then_inc(s_w, 16)
            act.dma_start(bd_sb[:], bd.rearrange("(o e) c -> o (e c)", o=1)).then_inc(s_w, 16)
            for half in range(2):
                act.dma_start(Wd_sb[:, half * 16:(half + 1) * 16, :],
                              Wd[half * 4:(half + 1) * 4].rearrange("e (k p) c -> p (e k) c", p=P)
                              ).then_inc(s_w, 16)

            def xT_out(G):
                act.wait_ge(s_xT, G.n + 1)
                if from_group(G, 2):
                    act.wait_ge(s_ei, H * (G.n - 1))
                act.activation(xTs[G.p][:], xT_ps[:], ACT.Copy).then_inc(s_xTs, 1)

            def exps(G):
                act.wait_ge(s_args, G.n + 1)
                act.activation(ex[G.p][:].rearrange("p t q h -> p (t q h)"),
                               args[G.p][:].rearrange("p t q h -> p (t q h)"), ACT.Exp).then_inc(s_ex, 1)

            def V_high(G):
                act.wait_ge(s_V, G.n + 1)
                if from_group(G, 2):
                    act.wait_ge(s_agg, Q * (G.n - 1))
                flat = "p q h t d -> p (q h t d)"
                act.activation(Vhi[G.p][:].rearrange(flat), V[G.p][:].rearrange(flat), ACT.Copy).then_inc(s_Vhi, 1)

            def exp_h(G):
                act.wait_ge(s_hh, G.n + 1)
                act.activation(eh_exp[G.p][:], hh[G.p][:], ACT.Exp).then_inc(s_eexp, 1)

            def steep_heads(heads):
                def body(G):
                    for h in heads:
                        act.wait_ge(s_ei, H * G.n + h + 1)
                        if h == 0:
                            act.wait_ge(s_eh, G.n + 1)
                        if from_group(G, 1) or h >= 2:
                            act.wait_ge(s_C, H * G.n + h - 1)
                        for b in range(GB):
                            for jt in range(JT):
                                last = act.activation(steep[h % 2][:, b, jt, :], ei_ps[h % 2][:, b * N:(b + 1) * N],
                                                      ACT.Relu, bias=eh[G.p][:, 2, JT * b + jt, h:h + 1], scale=STEEP)
                        last.then_inc(s_steep, 1)
                return body

            run_stages(act, GROUPS, 2, START1, [
                (2, steep_heads((0, 1))), (1, xT_out), (2, exps), (2, steep_heads((2,))), (2, V_high),
                (3, exp_h), (2, steep_heads((3,)))])

        @block.tensor
        def _(pe):
            pe.wait_ge(s_const, 5)
            pe.wait_ge(s_adjf, 1)
            for jt in range(JT):
                for it in range(JT):
                    last = pe.transpose(setup_ps[:, jt * N + it * P:jt * N + (it + 1) * P],
                                        adj_f[:, it, jt * P:(jt + 1) * P], ident[:])
            last.then_inc(s_adjT, 1)

            def transposes(G):
                pe.wait_ge(s_xn, G.n + 1)
                if from_group(G, 1):
                    pe.wait_ge(s_xTs, G.n)
                for q in range(Q):
                    last = pe.transpose(xT_ps[:, q * P:(q + 1) * P], xn[G.p][:, q, :], ident[:])
                last.then_inc(s_xT, 1)

            def project(G):
                pe.wait_ge(s_xTs, G.n + 1)
                if not from_group(G, 1):
                    pe.wait_ge(s_wa, 4)
                else:
                    pe.wait_ge(s_V, G.n)
                for q in range(Q):
                    c = (q % 2) * (F + 3 * H)
                    last = pe.matmul(Wh_ps[q // 2][:, c:c + F + 3 * H], xTs[G.p][:, q * P:(q + 1) * P],
                                     Wcat[:], start=True, stop=True)
                last.then_inc(s_wh, 1)

            def ei_heads(heads):
                def body(G):
                    for h in heads:
                        if from_group(G, 1) or h >= 2:
                            pe.wait_ge(s_steep, H * G.n + h - 1)
                        pe.matmul(ei_ps[h % 2][:], Wa1rep[:, h, :], xTs[G.p][:], start=True, stop=True
                                  ).then_inc(s_ei, 1)
                return body

            def sum_tiles(tiles):
                def body(G):
                    if 0 in tiles:
                        pe.wait_ge(s_C, H * (G.n + 1))
                        pe.wait_ge(s_Vlo, G.n + 1)
                    for q in tiles:
                        if from_group(G, 1) or q >= 2:
                            pe.wait_ge(s_num, Q * G.n + q - 1)
                        b, i_cols = q // JT, slice((q % JT) * P, (q % JT + 1) * P)
                        dst = agg_ps[q % 2][:, 0:H * 2 * D1].rearrange("p (h t d) -> p h t d", h=H, t=2)
                        parts = [(jt, v[G.p]) for jt in range(JT) for v in (Vhi, Vlo)]
                        for n, (jt, v) in enumerate(parts):
                            pe.matmul(dst[:, :, 1, :], negmask[:, jt, i_cols], v[:, JT * b + jt, :, 1, :],
                                      start=(n == 0), stop=False, skip_group_check=True)
                        for h in range(H):
                            for n, (jt, v) in enumerate(parts):
                                last = pe.matmul(dst[:, h, :, :].rearrange("p t d -> p (t d)"),
                                                 C[G.p][:, h, b, jt, i_cols],
                                                 v[:, JT * b + jt, h, :, :].rearrange("p t d -> p (t d)"),
                                                 start=False, stop=(h == H - 1 and n == 3),
                                                 skip_group_check=True)
                        last.then_inc(s_agg, 1)
                return body

            run_stages(pe, GROUPS, 2, START1, [
                (2, project), (2, ei_heads((0, 1))), (1, transposes), (3, sum_tiles((0, 1))),
                (2, ei_heads((2,))), (3, sum_tiles((2, 3))), (2, ei_heads((3,)))])

        @block.vector
        def _(dve):
            dve.wait_ge(s_adj, 16)
            dve.tensor_scalar(adj_f[:], adj_i[:], 0.0, None, ALU.is_gt).then_inc(s_adjf, 1)
            dve.wait_ge(s_w, 16 * WLOADS)
            Wv = Wcat[:, 0:F].rearrange("p (h d) -> p h d", h=H)
            for half in range(2):
                last = dve.tensor_tensor(wa_prod[:, half], Wv, a_sb[:, :, 1 - half, :], ALU.mult)
            last.then_inc(s_wa, 1)
            dve.wait_ge(s_wa, 1)
            dve.tensor_reduce(Wcat[:, F:F + 2 * H].rearrange("p (t h) -> p t h", t=2), wa_prod[:],
                              AX.X, ALU.add).then_inc(s_wa, 1)
            dve.wait_ge(s_wa, 2)
            dve.tensor_scalar(Wcat[:, F + 2 * H:], Wcat[:, F:F + H], STEEP, None, ALU.mult).then_inc(s_wa, 1)
            dve.tensor_copy(Wa1rep[:], Wcat[:, F + H:F + 2 * H].unsqueeze(2).broadcast_to([P, H, P])
                            ).then_inc(s_wa, 1)
            dve.wait_ge(s_adjT, 1)
            flat = "p t i -> p (t i)"
            dve.tensor_copy(mask[:].rearrange(flat), setup_ps[:])
            dve.tensor_scalar(negmask[:].rearrange(flat), setup_ps[:], -1.0, None, ALU.mult).then_inc(s_mask, 1)
            dve.wait_ge(s_mask, 1)
            dve.tensor_scalar(W1_hi[:], W1_sb[:], W_SCALE, None, ALU.mult).then_inc(s_mask, 1)
            dve.wait_ge(s_mask, 2)
            dve.scalar_tensor_tensor(W1_lo[:], W1_sb[:], W_SCALE, W1_hi[:], ALU.mult, ALU.subtract
                                     ).then_inc(s_mask, 1)

            def stats_of(G):
                dve.wait_ge(s_x[G.p], 16 * (G.k + 1))
                for q in range(Q):
                    last = dve.bn_stats(stats[G.p][:, q, :], x_all[:, bass.ds(G.n * Q + q, 1), 0:F].rearrange("p q f -> p (q f)"))
                last.then_inc(s_bn, 1)
                wait_apart(dve, s_bn, G.n + 1, s_passed)
                for q in range(Q):
                    last = dve.bn_aggr(mv[G.p][:, q, :], stats[G.p][:, q, :])
                last.then_inc(s_mv, 1)

            def normalise(G):
                dve.wait_ge(s_rstd, G.n + 1)
                if from_group(G, 2):
                    dve.wait_ge(s_xT, G.n - 1)
                for q in range(Q):
                    last = dve.tensor_scalar(xn[G.p][:, q, :], x_all[:, bass.ds(G.n * Q + q, 1), 0:F].rearrange("p q f -> p (q f)"),
                                             mv[G.p][:, q, 0:1], rstd[G.p][:, q:q + 1], ALU.subtract, ALU.mult)
                last.then_inc(s_xn, 1)

            def e_out(G):
                dve.wait_ge(s_wh, G.n + 1)
                for w in range(2):
                    src = Wh_ps[w][:, 0:2 * (F + 3 * H)].rearrange("p (q c) -> p q c", q=2)[:, :, F:]
                    last = dve.tensor_copy(eh[G.p][:, :, 2 * w:2 * w + 2, :],
                                           src.rearrange("p q (t h) -> p t q h", t=3))
                last.then_inc(s_eh, 1)
                dve.wait_ge(s_eh, G.n + 1)
                ev = eh[G.p][:, 0].rearrange("p (b t) h -> p t b h", b=GB)
                dve.tensor_tensor(emax[G.p][:], ev[:, 0], ev[:, 1], ALU.max).then_inc(s_emax, 1)

            def C_heads(heads):
                def body(G):
                    if 0 in heads and from_group(G, 2):
                        dve.wait_ge(s_agg, Q * (G.n - 1))
                    for h in heads:
                        dve.wait_ge(s_steep, H * G.n + h + 1)
                        dve.tensor_tensor(C[G.p][:, h].rearrange("p b t i -> p b (t i)"),
                                          steep[h % 2][:].rearrange("p b t i -> p b (t i)"),
                                          mask[:].rearrange("p t i -> p (t i)").unsqueeze(1).broadcast_to([P, GB, JT * N]),
                                          ALU.min).then_inc(s_C, 1)
                return body

            def V_out(G):
                dve.wait_ge(s_ex, G.n + 1)
                for w in range(2):
                    src = Wh_ps[w][:, 0:2 * (F + 3 * H)].rearrange("p (q c) -> p q c", q=2)[:, :, 0:F]
                    src = src.rearrange("p q (h d) -> p q h d", h=H)
                    for t in range(2):
                        dve.tensor_tensor(V[G.p][:, 2 * w:2 * w + 2, :, t, 0:D], src,
                                          ex[G.p][:, t, 2 * w:2 * w + 2, :].unsqueeze(3).broadcast_to([P, 2, H, D]),
                                          ALU.mult)
                dve.tensor_copy(V[G.p][:, :, :, :, D], ex[G.p][:, 0:2].rearrange("p t q h -> p q h t")
                                ).then_inc(s_V, 1)

            def divide(tiles):
                def body(G):
                    for q in tiles:
                        dve.wait_ge(s_agg, Q * G.n + q + 1)
                        src = agg_ps[q % 2][:, 0:H * 2 * D1].rearrange("p (h t d) -> p h t d", h=H, t=2)
                        dve.tensor_tensor(rB[:, q], src[:, :, 1, :],
                                          ex[G.p][:, 2, q, :].unsqueeze(2).broadcast_to([P, H, D1]), ALU.mult
                                          ).then_inc(s_rB, 1)
                        dve.wait_ge(s_rB, Q * G.n + q + 1)
                        dve.tensor_tensor(num[G.p][:, q], src[:, :, 0, :], rB[:, q], ALU.subtract
                                          ).then_inc(s_num, 1)
                return body

            def invert(G):
                dve.wait_ge(s_num, Q * (G.n + 1))
                dve.reciprocal(rden[G.p][:], num[G.p][:, :, :, D]).then_inc(s_rden, 1)

            def add_elu(G):
                if from_group(G, 1):
                    dve.wait_ge(s_x2, G.n)
                dve.wait_ge(s_xm1, G.n + 1)
                dve.wait_ge(s_hh, G.n + 1)
                dve.scalar_tensor_tensor(x_relu[:], hh[G.p][:], 0.0, xm1[G.p][:], ALU.max, ALU.add
                                         ).then_inc(s_relu, 1)
                dve.wait_ge(s_relu, G.n + 1)
                dve.wait_ge(s_eexp, G.n + 1)
                dve.scalar_tensor_tensor(x_all[:, bass.ds(G.n * Q, Q), 0:F], eh_exp[G.p][:], 1.0, x_relu[:],
                                         ALU.min, ALU.add).then_inc(s_x2, 1)

            run_stages(dve, GROUPS, 2, START1, [
                (1, normalise), (2, e_out), (0, stats_of), (2, C_heads((0,))), (3, divide((0, 1))),
                (2, C_heads((1,))), (3, divide((2, 3))), (3, invert), (2, V_out), (2, C_heads((2,))),
                (4, add_elu), (2, C_heads((3,)))])

        block1.__exit__(None, None, None)

        H_sb = [sb(f"H{i}", [P, KC, GT]) for i in range(3)]
        h_ps = bank[1:5]
        gate_ps = bank[5]
        rank_ps = bank[6]
        total_ps = bank[7]
        xT_hi = [sb(f"xT_hi{i}", [P, GT], F16) for i in range(3)]
        xT_lo = [sb(f"xT_lo{i}", [P, GT], F16) for i in range(3)]
        iota_e = sb("iota_e", [P, E])
        base_e = sb("base_e", [P, E])
        euler = sb("euler", [P, Q, E])
        before = sb("before", [P, P], F16)
        ones16 = sb("ones16", [P, P], F16)
        meta = sb("meta", [P, TILES, 4])
        mr = [sb(f"mr{i}", [P, Q, 2]) for i in range(2)]
        lg = sb("lg", [P, Q, E])
        top = sb("top", [P, Q])
        below = [sb(f"below{i}", [P, Q, E]) for i in range(2)]
        is_top = sb("is_top", [P, Q, E])
        cand = sb("cand", [P, Q, E])
        first = sb("first", [P, Q])
        hot = [sb(f"hot{i}", [P, Q, E], F16) for i in range(2)]
        hot_sum = [sb(f"hot_sum{i}", [P, Q, E], F16) for i in range(2)]
        exps2 = [sb(f"exps2{i}", [P, Q, E]) for i in range(2)]
        total = sb("total", [P, Q])
        ranked = sb("ranked", [P, Q, E])
        masked = sb("masked", [P, Q, E])
        place = [sb(f"place{i}", [P, Q], U32) for i in range(2)]
        place_f = sb("place_f", [P, Q])
        rows = [sb(f"rows{i}", [P, Q, ROW]) for i in range(2)]
        nobody = sb("nobody", [P, ROW])

        s2_const = sem("p2_constants")
        s2_bn = sem("p2_stats_of_tiles")
        s2_mv = sem("p2_mean_var_ready")
        s2_veps = sem("p2_var_eps")
        s2_rstd = sem("p2_rstd_ready")
        s2_meta = sem("p2_meta_kept")
        s2_xn = sem("p2_normalised")
        s2_xT = sem("p2_transposed")
        s2_hi = sem("p2_high_part")
        s2_lo = sem("p2_low_part")
        s2_h = sem("p2_hidden_chunks")
        s2_gelu = sem("p2_gelu_chunks")
        s2_gate = sem("p2_gate_logits")
        s2_top = sem("p2_top_chain")
        s2_below = sem("p2_logits_below_top")
        s2_hot = sem("p2_onehot_ready")
        s2_sum = sem("p2_onehot_sums")
        s2_exp = sem("p2_exps_ready")
        s2_rank = sem("p2_ranks_ready")
        s2_ranked = sem("p2_ranks_chain")
        s2_place = sem("p2_places_ready")
        s2_x = sem("p2_x_in_rows")
        s2_rows = sem("p2_rows_ready")
        s2_put = [sem("p2_rows_stored0"), sem("p2_rows_stored1")]
        s2_nobody = sem("p2_nobody_stored")
        START2 = 6

        with nc.Block() as block:
            @block.sync
            def _(sp):
                sp.wait_ge(s2_const, 9)
                sp.dma_start(lists[E * LIST:E * LIST + P, :], nobody[:]).then_inc(s2_nobody, 16)
                sp.wait_ge(s2_nobody, 16)

            @block.gpsimd
            def _(pool):
                pool.memset(nobody[:], 0.0).then_inc(s2_const, 1)
                pool.memset(euler[:], 2.718281828459045).then_inc(s2_const, 1)
                pool.memset(ones16[:], 1.0).then_inc(s2_const, 1)
                pool.memset(hot_sum[0][:], 0.0).then_inc(s2_const, 1)
                pool.iota(iota_e[:], pattern=[[1, E]], base=-E, channel_multiplier=0,
                          allow_small_or_imprecise_dtypes=True).then_inc(s2_const, 1)
                pool.iota(base_e[:], pattern=[[LIST, E]], base=0, channel_multiplier=0,
                          allow_small_or_imprecise_dtypes=True).then_inc(s2_const, 1)
                pool.iota(meta[:, :, 3], pattern=[[P, TILES]], base=0, channel_multiplier=1,
                          allow_small_or_imprecise_dtypes=True).then_inc(s2_const, 1)
                pool.wait_ge(s2_const, 7)
                pool.memset(nobody[:, ROW - 1:ROW], float(NOBODY)).then_inc(s2_const, 1)
                pool.affine_select(out=before[:], in_=ones16[:], compare_op=ALU.is_gt, fill=0.0, base=0,
                                   pattern=[[1, P]], channel_multiplier=-1).then_inc(s2_const, 1)

                def rstd_of(G):
                    wait_apart(pool, s2_mv, G.n + 1, s_passed)
                    pool.tensor_scalar(veps[G.p][:], mv[G.p][:, :, 1], EPS, None, ALU.add).then_inc(s2_veps, 1)
                    pool.tensor_copy(mr[G.p][:, :, 0], mv[G.p][:, :, 0])
                    pool.wait_ge(s2_veps, G.n + 1)
                    pool.tensor_tensor(mr[G.p][:, :, 1], veps[G.p][:], mhalf[:], ALU.pow).then_inc(s2_rstd, 1)
                    pool.wait_ge(s2_rstd, G.n + 1)
                    pool.tensor_copy(meta[:, bass.ds(G.n * Q, Q), 0:2], mr[G.p][:]).then_inc(s2_meta, 1)

                def sum_up(G):
                    pool.wait_ge(s2_hot, G.n + 1)
                    for q in range(Q):
                        dst = hot_sum[G.p][:, q + 1, :] if q < Q - 1 else hot_sum[1 - G.p][:, 0, :]
                        pool.tensor_tensor(dst, hot_sum[G.p][:, q, :], hot[G.p][:, q, :], ALU.add).then_inc(s2_sum, 1)
                        if q < Q - 1:
                            pool.wait_ge(s2_sum, Q * G.n + q + 1)
                    pool.tensor_tensor(exps2[G.p][:], euler[:], below[G.p][:], ALU.pow).then_inc(s2_exp, 1)

                def put(G):
                    pool.wait_ge(s2_place, G.n + 1)
                    pool.tensor_copy(rows[G.p][:, :, F:ROW], meta[:, bass.ds(G.n * Q, Q), :]).then_inc(s2_rows, 1)
                    wait_apart(pool, s2_x, G.n + 1, s_passed)
                    wait_apart(pool, s2_rows, G.n + 1, s_passed)
                    for q in range(Q):
                        pool.indirect_dma_start(
                            out=lists[:, :], out_offset=bass.IndirectOffsetOnAxis(ap=place[G.p][:, q:q + 1], axis=0),
                            in_=rows[G.p][:, q, :], in_offset=None).then_inc(s2_put[G.p], 16)

                run_stages(pool, GROUPS, 2, START2, [(0, rstd_of), (3, sum_up), (4, put)])
                for i in range(2):
                    pool.wait_ge(s2_put[i], 16 * Q * GROUPS // 2)

            @block.scalar
            def _(act):
                def high_part(G):
                    act.wait_ge(s2_xT, G.n + 1)
                    if from_group(G, 2):
                        act.wait_ge(s2_h, KC * (G.n - 1))
                    act.activation(xT_hi[G.p][:], xT_ps[:], ACT.Copy).then_inc(s2_hi, 1)

                def gelu(G):
                    if from_group(G, 2):
                        act.wait_ge(s2_gate, G.n - 1)
                    for k in range(KC):
                        act.wait_ge(s2_h, KC * G.n + k + 1)
                        act.activation(H_sb[G.p][:, k, :], h_ps[k][:], ACT.Gelu, bias=b1_sb[:, k:k + 1],
                                       scale=1.0 / W_SCALE).then_inc(s2_gelu, 1)

                def x_in_rows(G):
                    if from_group(G, 2):
                        act.wait_ge(s2_put[G.p], 16 * Q * G.k)
                    act.activation(rows[G.p][:, :, 0:F], x_all[:, bass.ds(G.n * Q, Q), :], ACT.Copy).then_inc(s2_x, 1)

                run_stages(act, GROUPS, 2, START2, [(1, high_part), (4, x_in_rows), (2, gelu)])

            @block.tensor
            def _(pe):
                def transposes(G):
                    pe.wait_ge(s2_xn, G.n + 1)
                    if from_group(G, 1):
                        pe.wait_ge(s2_lo, G.n)
                    for q in range(Q):
                        last = pe.transpose(xT_ps[:, q * P:(q + 1) * P], xn[G.p][:, q, :], ident[:])
                    last.then_inc(s2_xT, 1)

                def hidden(G):
                    pe.wait_ge(s2_lo, G.n + 1)
                    for k in range(KC):
                        cols = slice(k * P, (k + 1) * P)
                        if from_group(G, 1):
                            pe.wait_ge(s2_gelu, KC * (G.n - 1) + k + 1)
                        pe.matmul(h_ps[k][:], W1_hi[:, cols], xT_lo[G.p][:], start=True, stop=False)
                        pe.matmul(h_ps[k][:], W1_lo[:, cols], xT_hi[G.p][:], start=False, stop=False)
                        pe.matmul(h_ps[k][:], W1_hi[:, cols], xT_hi[G.p][:], start=False, stop=True).then_inc(s2_h, 1)

                def gate(G):
                    pe.wait_ge(s2_gelu, KC * (G.n + 1))
                    if from_group(G, 1):
                        pe.wait_ge(s2_top, 5 * (G.n - 1) + 1)
                    for q in range(Q):
                        for k in range(KC):
                            last = pe.matmul(gate_ps[:, q * E:(q + 1) * E], H_sb[G.p][:, k, q * P:(q + 1) * P],
                                             Wg_sb[:, k, :], start=(k == 0), stop=(k == KC - 1))
                    last.then_inc(s2_gate, 1)

                def rank(G):
                    pe.wait_ge(s2_sum, Q * (G.n + 1))
                    if from_group(G, 1):
                        pe.wait_ge(s2_ranked, 3 * (G.n - 1) + 1)
                    flat = "p q e -> p (q e)"
                    pe.matmul(rank_ps[:, 0:Q * E], before[:], hot[G.p][:].rearrange(flat), start=True, stop=False)
                    pe.matmul(rank_ps[:, 0:Q * E], ones16[:], hot_sum[G.p][:].rearrange(flat),
                              start=False, stop=True).then_inc(s2_rank, 1)

                pe.wait_ge(s2_const, 9)
                run_stages(pe, GROUPS, 2, START2, [(3, gate), (1, transposes), (2, hidden), (3, rank)])
                pe.matmul(total_ps[:, 0:E], ones16[:], hot_sum[GROUPS % 2][:, 0, :], start=True, stop=True)

            @block.vector
            def _(dve):
                def stats_of(G):
                    if from_group(G, 2):
                        dve.wait_ge(s2_meta, G.n - 1)
                    for q in range(Q):
                        last = dve.bn_stats(stats[G.p][:, q, :],
                                            x_all[:, bass.ds(G.n * Q + q, 1), :].rearrange("p q f -> p (q f)"))
                    last.then_inc(s2_bn, 1)
                    wait_apart(dve, s2_bn, G.n + 1, s_passed)
                    for q in range(Q):
                        last = dve.bn_aggr(mv[G.p][:, q, :], stats[G.p][:, q, :])
                    last.then_inc(s2_mv, 1)

                def normalise(G):
                    dve.wait_ge(s2_rstd, G.n + 1)
                    if from_group(G, 2):
                        dve.wait_ge(s2_xT, G.n - 1)
                    for q in range(Q):
                        last = dve.tensor_scalar(xn[G.p][:, q, :],
                                                 x_all[:, bass.ds(G.n * Q + q, 1), :].rearrange("p q f -> p (q f)"),
                                                 mr[G.p][:, q, 0:1], mr[G.p][:, q, 1:2], ALU.subtract, ALU.mult)
                    last.then_inc(s2_xn, 1)

                def low_part(G):
                    dve.wait_ge(s2_hi, G.n + 1)
                    dve.tensor_tensor(xT_lo[G.p][:], xT_ps[:], xT_hi[G.p][:], ALU.subtract).then_inc(s2_lo, 1)

                def over_e(ap):
                    return ap.unsqueeze(2).broadcast_to([P, Q, E])

                def over_q(ap):
                    return ap.unsqueeze(1).broadcast_to([P, Q, E])

                def choose(G):
                    base = 5 * G.n
                    dve.wait_ge(s2_gate, G.n + 1)
                    dve.tensor_tensor(lg[:], gate_ps[:, 0:Q * E].rearrange("p (q e) -> p q e", q=Q),
                                      over_q(bg_sb[:]), ALU.add).then_inc(s2_top, 1)
                    dve.wait_ge(s2_top, base + 1)
                    dve.tensor_reduce(top[:], lg[:], AX.X, ALU.max).then_inc(s2_top, 1)
                    dve.wait_ge(s2_top, base + 2)
                    if from_group(G, 2):
                        dve.wait_ge(s2_exp, G.n - 1)
                    dve.tensor_tensor(below[G.p][:], lg[:], over_e(top[:]), ALU.subtract).then_inc(s2_below, 1)
                    dve.wait_ge(s2_below, G.n + 1)
                    dve.tensor_scalar(is_top[:], below[G.p][:], 0.0, None, ALU.is_equal).then_inc(s2_top, 1)
                    dve.wait_ge(s2_top, base + 3)
                    dve.tensor_tensor(cand[:], is_top[:], over_q(iota_e[:]), ALU.mult).then_inc(s2_top, 1)
                    dve.wait_ge(s2_top, base + 4)
                    dve.tensor_reduce(first[:], cand[:], AX.X, ALU.min).then_inc(s2_top, 1)
                    dve.wait_ge(s2_top, base + 5)
                    if from_group(G, 2):
                        dve.wait_ge(s2_rank, G.n - 1)
                    dve.tensor_tensor(hot[G.p][:], over_q(iota_e[:]), over_e(first[:]), ALU.is_equal).then_inc(s2_hot, 1)

                def places(G):
                    dve.wait_ge(s2_rank, G.n + 1)
                    dve.tensor_tensor(ranked[:], rank_ps[:, 0:Q * E].rearrange("p (q e) -> p q e", q=Q),
                                      over_q(base_e[:]), ALU.add).then_inc(s2_ranked, 1)
                    dve.wait_ge(s2_exp, G.n + 1)
                    dve.tensor_reduce(total[:], exps2[G.p][:], AX.X, ALU.add)
                    dve.wait_ge(s2_ranked, 3 * G.n + 1)
                    dve.tensor_tensor(masked[:], ranked[:], hot[G.p][:], ALU.mult).then_inc(s2_ranked, 1)
                    dve.wait_ge(s2_ranked, 3 * G.n + 2)
                    if from_group(G, 2):
                        dve.wait_ge(s2_rows, G.n - 1)
                    dve.reciprocal(meta[:, bass.ds(G.n * Q, Q), 2], total[:])
                    dve.tensor_reduce(place_f[:], masked[:], AX.X, ALU.add).then_inc(s2_ranked, 1)
                    dve.wait_ge(s2_ranked, 3 * G.n + 3)
                    if from_group(G, 2):
                        dve.wait_ge(s2_put[G.p], 16 * Q * G.k)
                    dve.tensor_copy(place[G.p][:], place_f[:]).then_inc(s2_place, 1)

                dve.wait_ge(s2_const, 9)
                run_stages(dve, GROUPS, 2, START2, [(4, places), (1, normalise), (0, stats_of), (1, low_part), (3, choose)])

        iota_p = sb("iota_p", [P, 1])
        slot_f = sb("slot_f", [1, SLOTS])
        count = sb("count", [P, E])
        count_i = sb("count_i", [P, E], I32)
        blocks_i = sb("blocks_i", [P, E], I32)
        blocks_f = sb("blocks_f", [P, E])
        cum = [sb(f"cum{i}", [P, E]) for i in range(2)]
        room = sb("room", [1, E])
        tail_f = sb("tail_f", [P, E])
        tail_u = sb("tail_u", [P, E], U32)
        past = sb("past", [1, SLOTS, E])
        jumps = sb("jumps", [1, SLOTS, E])
        expert_f = sb("expert_f", [1, SLOTS])
        expert_i = sb("expert_i", [1, SLOTS], I32)
        start_f = sb("start_f", [1, SLOTS])
        start_i = sb("start_i", [1, SLOTS], I32)

        s3_const = sem("p3_constants")
        s3 = sem("p3_vector_step")
        s3_tail = sem("p3_tails_ready")
        s3_fill = sem("p3_tails_stored")

        with nc.Block() as block:
            @block.gpsimd
            def _(pool):
                pool.iota(iota_p[:], pattern=[[1, 1]], base=0, channel_multiplier=1,
                          allow_small_or_imprecise_dtypes=True).then_inc(s3_const, 1)
                pool.iota(slot_f[:], pattern=[[P, SLOTS]], base=0, channel_multiplier=0,
                          allow_small_or_imprecise_dtypes=True).then_inc(s3_const, 1)
                pool.wait_ge(s3_tail, 1)
                for e in range(E):
                    pool.indirect_dma_start(
                        out=lists[:, :], out_offset=bass.IndirectOffsetOnAxis(ap=tail_u[:, e:e + 1], axis=0),
                        in_=nobody[:], in_offset=None).then_inc(s3_fill, 16)
                pool.wait_ge(s3_fill, 16 * E)

            @block.vector
            def _(dve):
                steps = [0]

                def step(instruction):
                    steps[0] += 1
                    instruction.then_inc(s3, 1)
                    dve.wait_ge(s3, steps[0])

                dve.wait_ge(s3_const, 2)
                step(dve.tensor_copy(count[:], total_ps[:, 0:E]))
                step(dve.scalar_tensor_tensor(tail_f[:], count[:], iota_p[:], base_e[:], ALU.add, ALU.add))
                dve.tensor_copy(tail_u[:], tail_f[:]).then_inc(s3_tail, 1)
                step(dve.tensor_scalar(count_i[:], count[:], float(P - 1), None, ALU.add))
                step(dve.tensor_scalar(blocks_i[:], count_i[:], P.bit_length() - 1, None, ALU.arith_shift_right))
                step(dve.tensor_scalar(blocks_f[:], blocks_i[:], float(P), None, ALU.mult))
                step(dve.tensor_scalar(room[:], blocks_f[0:1, :], -1.0, float(LIST), ALU.mult, ALU.add))
                step(dve.tensor_copy(cum[0][:], blocks_f[:]))
                n = 0
                for shift in (1, 2, 4):
                    dve.tensor_copy(cum[1 - n][:, 0:shift], cum[n][:, 0:shift])
                    step(dve.tensor_tensor(cum[1 - n][:, shift:], cum[n][:, shift:], cum[n][:, 0:E - shift], ALU.add))
                    n = 1 - n
                step(dve.tensor_tensor(past[:], cum[n][0:1, :].unsqueeze(1).broadcast_to([1, SLOTS, E]),
                                       slot_f[:].unsqueeze(2).broadcast_to([1, SLOTS, E]), ALU.is_le))
                dve.tensor_reduce(expert_f[:], past[:], AX.X, ALU.add)
                step(dve.tensor_tensor(jumps[:], past[:], room[:].unsqueeze(1).broadcast_to([1, SLOTS, E]), ALU.mult))
                step(dve.tensor_reduce(start_f[:], jumps[:], AX.X, ALU.add))
                step(dve.tensor_tensor(start_f[:], start_f[:], slot_f[:], ALU.add))
                step(dve.tensor_scalar(start_i[:], start_f[:], float(E * LIST), None, ALU.min))
                dve.tensor_scalar(expert_i[:], expert_f[:], float(E - 1), None, ALU.min)

        NB4 = 3
        idx_out = [sb(f"idx_out{i}", [P, Q], U32) for i in range(NB4)]
        xg = [sb(f"xg{i}", [P, Q, ROW]) for i in range(NB4)]
        xn4 = [sb(f"xn4_{i}", [P, Q, F]) for i in range(NB4)]
        yo = [sb(f"yo{i}", [P, Q, F]) for i in range(NB4)]
        y_ps = bank[5:8]
        s4_in = [sem(f"p4_rows_loaded{i}") for i in range(NB4)]
        s4_xn = sem("p4_normalised")
        s4_xT = sem("p4_transposed")
        s4_hi = sem("p4_high_part")
        s4_lo = sem("p4_low_part")
        s4_h = sem("p4_hidden_chunks")
        s4_gelu = sem("p4_gelu_chunks")
        s4_y = sem("p4_expert_tiles")
        s4_yo = sem("p4_rows_ready")
        s4_out = [sem(f"p4_rows_stored{i}") for i in range(NB4)]
        START4 = 6

        with nc.Block() as block:
            @block.sync
            def _(sp):
                def load(G):
                    if from_group(G, 3):
                        sp.wait_ge(s4_yo, G.n - 2)
                    for q in range(Q):
                        start = sp.value_load(start_i[0:1, bass.ds(G.n * Q + q, 1)], min_val=0, max_val=E * LIST)
                        sp.dma_start(xg[G.p][:, q, :], lists[bass.ds(start, P), :]).then_inc(s4_in[G.p], 16)

                run_stages(sp, SGROUPS, NB4, 3, [(0, load)])

            @block.gpsimd
            def _(pool):
                def scatter(G):
                    wait_apart(pool, s4_yo, G.n + 1, s_passed)
                    for q in range(Q):
                        pool.indirect_dma_start(
                            out=out[:, :], out_offset=bass.IndirectOffsetOnAxis(ap=idx_out[G.p][:, q:q + 1], axis=0),
                            in_=yo[G.p][:, q, :], in_offset=None, bounds_check=B * N - 1, oob_is_err=False
                        ).then_inc(s4_out[G.p], 16)

                run_stages(pool, SGROUPS, NB4, 3, [(0, scatter)])
                for i in range(NB4):
                    pool.wait_ge(s4_out[i], 16 * Q * SGROUPS // NB4)

            @block.scalar
            def _(act):
                def high_part(G):
                    act.wait_ge(s4_xT, G.n + 1)
                    if from_group(G, 3):
                        act.wait_ge(s4_h, KC * (G.n - 2))
                    act.activation(xT_hi[G.p][:], xT_ps[:], ACT.Copy).then_inc(s4_hi, 1)

                def gelu(G):
                    if from_group(G, 3):
                        act.wait_ge(s4_y, Q * (G.n - 2))
                    for k in range(KC):
                        act.wait_ge(s4_h, KC * G.n + k + 1)
                        act.activation(H_sb[G.p][:, k, :], h_ps[k][:], ACT.Gelu, bias=b1_sb[:, k:k + 1],
                                       scale=1.0 / W_SCALE).then_inc(s4_gelu, 1)

                run_stages(act, SGROUPS, NB4, START4, [(1, high_part), (1, gelu)])

            @block.tensor
            def _(pe):
                def transposes(G):
                    pe.wait_ge(s4_xn, G.n + 1)
                    if from_group(G, 1):
                        pe.wait_ge(s4_lo, G.n)
                    for q in range(Q):
                        last = pe.transpose(xT_ps[:, q * P:(q + 1) * P], xn4[G.p][:, q, :], ident[:])
                    last.then_inc(s4_xT, 1)

                def hidden(G):
                    pe.wait_ge(s4_lo, G.n + 1)
                    for k in range(KC):
                        cols = slice(k * P, (k + 1) * P)
                        if from_group(G, 1):
                            pe.wait_ge(s4_gelu, KC * (G.n - 1) + k + 1)
                        pe.matmul(h_ps[k][:], W1_hi[:, cols], xT_lo[G.p][:], start=True, stop=False)
                        pe.matmul(h_ps[k][:], W1_lo[:, cols], xT_hi[G.p][:], start=False, stop=False)
                        pe.matmul(h_ps[k][:], W1_hi[:, cols], xT_hi[G.p][:], start=False, stop=True).then_inc(s4_h, 1)

                def experts(G):
                    e = [pe.value_load(expert_i[0:1, bass.ds(G.n * Q + q, 1)], min_val=0, max_val=E - 1)
                         for q in range(Q)]
                    pe.wait_ge(s4_gelu, KC * (G.n + 1))
                    if from_group(G, 3):
                        pe.wait_ge(s4_yo, G.n - 2)
                    for q in range(Q):
                        y = y_ps[G.p][:, q * F:(q + 1) * F]
                        for k in range(KC):
                            pe.matmul(y, H_sb[G.p][:, k, q * P:(q + 1) * P],
                                      Wd_sb[:, bass.ds(e[q] * KC + k, 1), :].rearrange("p o c -> p (o c)"),
                                      start=(k == 0), stop=False)
                        pe.matmul(y, ones_row[:], bd_sb[:, bass.ds(e[q] * F, F)], start=False, stop=True
                                  ).then_inc(s4_y, 1)

                run_stages(pe, SGROUPS, NB4, START4, [(1, transposes), (2, experts), (1, hidden)])

            @block.vector
            def _(dve):
                def normalise(G):
                    dve.wait_ge(s4_in[G.p], 16 * Q * (G.k + 1))
                    if from_group(G, 3):
                        dve.wait_ge(s4_xT, G.n - 2)
                    for q in range(Q):
                        last = dve.tensor_scalar(xn4[G.p][:, q, :], xg[G.p][:, q, 0:F], xg[G.p][:, q, F:F + 1],
                                                 xg[G.p][:, q, F + 1:F + 2], ALU.subtract, ALU.mult)
                    last.then_inc(s4_xn, 1)

                def low_part(G):
                    dve.wait_ge(s4_hi, G.n + 1)
                    dve.tensor_tensor(xT_lo[G.p][:], xT_ps[:], xT_hi[G.p][:], ALU.subtract).then_inc(s4_lo, 1)

                def combine(G):
                    if from_group(G, 3):
                        dve.wait_ge(s4_out[G.p], 16 * Q * G.k)
                    dve.tensor_copy(idx_out[G.p][:], xg[G.p][:, :, ROW - 1])
                    dve.wait_ge(s4_y, Q * (G.n + 1))
                    for q in range(Q):
                        last = dve.scalar_tensor_tensor(
                            yo[G.p][:, q, :], y_ps[G.p][:, q * F:(q + 1) * F],
                            xg[G.p][:, q, F + 2:F + 3], xg[G.p][:, q, 0:F], ALU.mult, ALU.add)
                    last.then_inc(s4_yo, 1)

                run_stages(dve, SGROUPS, NB4, START4, [(1, normalise), (1, low_part), (2, combine)])


_INS = ["x", "adj", "L0_gnn_W", "L0_gnn_a", "L0_ffn_W1", "L0_ffn_b1", "L0_ffn_Wg", "L0_ffn_bg",
        "L0_ffn_Wd", "L0_ffn_bd"]


def kernel(**inputs):
    import numpy as np
    import concourse.bacc as bacc
    from concourse.bass_utils import run_bass_kernel_spmd

    nc = bacc.Bacc("TRN2", target_bir_lowering=False, num_devices=1)
    arrays, args = {}, []
    for name in _INS:
        v = np.ascontiguousarray(inputs[name])
        if name == "x":
            v = v.reshape(B * N, F)
        arrays[f"in_{name}"] = v
        args.append(nc.dram_tensor(f"in_{name}", v.shape, mybir.dt.from_np(v.dtype), kind="ExternalInput").ap())
    out = nc.dram_tensor("out", (B * N, F), F32, kind="ExternalOutput").ap()
    build(nc, *args, out)
    r = run_bass_kernel_spmd(nc, [arrays], core_ids=[0])
    return r.results[0]["out"].reshape(B, N, F)
```

```python
from collections import namedtuple
from contextlib import ExitStack

import concourse.bass as bass
from concourse import mybir

ALU = mybir.AluOpType
ACT = mybir.ActivationFunctionType
AX = mybir.AxisListType
F32 = mybir.dt.float32
F16 = mybir.dt.float16
BF16 = mybir.dt.bfloat16
I32 = mybir.dt.int32
U32 = mybir.dt.uint32
MAX = bass.bass_isa.ReduceOp.max

P = 128
BANK = 512
B, N, F = 32, 256, 128
H, D = 4, 32
HID, E = 512, 8
KC = HID // P
TILES = B * N // P
Q = 4
GT = Q * P
GROUPS = TILES // Q
GB = GT // N
JT = N // P
D1 = D + 1
EPS = 1e-5
SCALE_LN = 10 * 0.6931471805599453
START1 = 6
SLOTS = TILES + E
SGROUPS = SLOTS // Q
LIST = B * N + P
NOBODY = B * N
ROW = F + 4
STEEP = 2.0 ** 100
LO = 32
W_SCALE = 2.0 ** 8

Group = namedtuple("Group", "n k p")


def run_stages(eng, groups, buffers, start, stages):
    last = max(lag for lag, _ in stages)

    def peeled(t):
        for lag, body in stages:
            n = t - lag
            if 0 <= n < groups:
                body(Group(n, n // buffers, n % buffers))

    for t in range(start):
        peeled(t)
    with eng.Fori(start // buffers, groups // buffers) as i:
        for u in range(buffers):
            for lag, body in stages:
                body(Group(buffers * i + (u - lag), i + (u - lag) // buffers, (u - lag) % buffers))
    for t in range(groups, groups + last):
        peeled(t)


def from_group(G, first):
    return not isinstance(G.n, int) or G.n >= first


def wait_apart(eng, sem, value, passed):
    eng.wait_ge(sem, value)
    eng.sem_inc(passed, 1)


def build(nc, x, adj, W, a, W1, b1, Wg, bg, Wd, bd, out):
    ctx = ExitStack()
    with ctx:
        def sb(name, shape, dt=F32):
            return ctx.enter_context(nc.sbuf_tensor(name, shape, dt))

        phase1 = ctx.enter_context(ExitStack())

        def sb1(name, shape, dt=F32):
            return phase1.enter_context(nc.sbuf_tensor(name, shape, dt))

        def sem(name):
            return ctx.enter_context(nc.semaphore(name))

        lists = nc.dram_tensor("lists", (E * LIST + P, ROW), F32, kind="Internal").ap()

        x_all = sb("x_all", [P, TILES, F])
        ident = sb("ident", [P, P])
        Wd_sb = sb("Wd_sb", [P, E * KC, F])
        Wd_hi = sb("Wd_hi", [P, E * KC, F], F16)
        Wd_lo = sb("Wd_lo", [P, E * KC, F], F16)
        bd_sb = sb("bd_sb", [LO + 1, E * KC, F // KC])
        bd2 = sb("bd2", [LO + 1, E * KC, F // KC], F16)
        W1_sb = sb("W1_sb", [P, HID])
        b1_sb = sb("b1_sb", [P, KC])
        Wg_sb = sb("Wg_sb", [P, KC, E])
        bg_sb = sb("bg_sb", [P, E])
        mhalf = sb("mhalf", [P, Q])
        ones = sb("ones", [P, Q, F])
        W1_hi = sb("W1_hi", [P, HID], F16)
        W1_lo = sb("W1_lo", [P, HID], F16)
        stats = [sb(f"stats{i}", [P, Q, 6]) for i in range(2)]
        mv = [sb(f"mv{i}", [P, Q, 2]) for i in range(2)]
        veps = [sb(f"veps{i}", [P, Q]) for i in range(2)]
        rstd = [sb(f"rstd{i}", [P, Q]) for i in range(2)]
        xn = [sb(f"xn{i}", [P, Q, F]) for i in range(2)]
        adj_i = sb1("adj_i", [P, JT, N], I32)
        adj_f = sb1("adj_f", [P, JT, N])
        mask = sb1("mask", [P, JT, N], BF16)
        negmask = sb1("negmask", [P, JT, N], BF16)
        a_sb = sb1("a_sb", [P, H, 2, D])
        wa_prod = sb1("wa_prod", [P, 2, H, D])
        Wcat = sb1("Wcat", [P, F + 3 * H])
        Wa1rep = sb1("Wa1rep", [P, H, P])
        xTs = [sb1(f"xTs{i}", [P, GT]) for i in range(2)]
        eh = [sb1(f"eh{i}", [P, 3, Q, H]) for i in range(2)]
        emax = [sb1(f"emax{i}", [P, GB, H]) for i in range(2)]
        guard = [sb1(f"guard{i}", [P, GB, H]) for i in range(2)]
        shifted = [sb1(f"shifted{i}", [P, 2, Q, H]) for i in range(2)]
        args = [sb1(f"args{i}", [P, 3, Q, H]) for i in range(2)]
        ex = [sb1(f"ex{i}", [P, 3, Q, H]) for i in range(2)]
        V = [sb1(f"V{i}", [P, Q, H, 2, D1]) for i in range(2)]
        Vhi = [sb1(f"Vhi{i}", [P, Q, H, 2, D1], F16) for i in range(2)]
        Vlo = [sb1(f"Vlo{i}", [P, Q, H, 2, D1], F16) for i in range(2)]
        steep = [sb1(f"steep{i}", [P, GB, JT, N], BF16) for i in range(2)]
        C = [sb1(f"C{i}", [P, H, GB, JT, N], BF16) for i in range(2)]
        rB = sb1("rB", [P, Q, H, D1])
        num = [sb1(f"num{i}", [P, Q, H, D1]) for i in range(2)]
        rden = [sb1(f"rden{i}", [P, Q, H]) for i in range(2)]
        hh = [sb1(f"hh{i}", [P, Q, F]) for i in range(2)]
        eh_exp = [sb1(f"eh_exp{i}", [P, Q, F]) for i in range(2)]
        xm1 = [sb1(f"xm1{i}", [P, Q, F]) for i in range(2)]
        x_relu = sb1("x_relu", [P, Q, F])

        psum = ctx.enter_context(nc.psum_tensor("psum", [P, 8, BANK], F32))
        bank = [psum[:, i, :] for i in range(8)]
        xT_ps = bank[0]
        Wh_ps = psum[:, 1:3, :].rearrange("p b (t c) -> p (b t) c", t=2)
        ei_ps = [bank[3], bank[4], bank[3], bank[7]]
        agg_ps = psum[:, 5:7, 0:H * 2 * D1].rearrange("p b (h t d) -> p b h t d", h=H, t=2)
        setup_ps = bank[7]

        s_w = sem("weights_loaded")
        s_passed = sem("waits_passed")
        s_adj = sem("adj_loaded")
        s_x = [sem("x_loaded0"), sem("x_loaded1")]
        s_const = sem("constants_ready")
        s_bd = sem("bd_cleared")
        s_adjf = sem("adj_float")
        s_adjT = sem("adj_transposed")
        s_mask = sem("mask_ready")
        s_wa = sem("wa_ready")
        s_bn = sem("stats_of_tiles")
        s_mv = sem("mean_var_ready")
        s_veps = sem("var_eps")
        s_rstd = sem("rstd_ready")
        s_xn = sem("normalised")
        s_xT = sem("transposed")
        s_xTs = sem("transposed_in_sbuf")
        s_wh = sem("wh_ready")
        s_ei = sem("ei_broadcast")
        s_eh = sem("e_in_sbuf")
        s_emax = sem("e_max_of_tiles")
        s_guard = sem("guard_ready")
        s_shift = sem("e_shifted")
        s_clamp = sem("ei_clamped")
        s_args = sem("exp_args_ready")
        s_ex = sem("exps_ready")
        s_V = sem("V_ready")
        s_Vhi = sem("V_high_part")
        s_Vlo = sem("V_low_part")
        s_steep = sem("steep_of_heads")
        s_C = sem("C_of_heads")
        s_agg = sem("sums_of_tiles")
        s_rB = sem("rB_of_tiles")
        s_num = sem("numerators_of_tiles")
        s_rden = sem("denominator_inverted")
        s_hh = sem("h_ready")
        s_eexp = sem("exp_h_ready")
        s_xm1 = sem("x_minus_1")
        s_relu = sem("x_plus_relu")
        s_x2 = sem("x2_ready")

        block1 = nc.Block()
        block = block1.__enter__()

        WLOADS = 10

        @block.sync
        def _(sp):
            sp.dma_start(adj_i[:], adj.rearrange("(t p) j -> p t j", p=P)).then_inc(s_adj, 16)
            with nc.allow_non_contiguous_dma(reason="small weights, once"):
                sp.dma_start(Wcat[:, 0:F].rearrange("p (h d) -> p h d", h=H),
                             W.rearrange("h f d -> f h d")).then_inc(s_w, 16)
                sp.dma_start(a_sb[:].rearrange("p h t d -> p (h t d)"),
                             a.rearrange("h t -> (h t)").partition_broadcast(P)).then_inc(s_w, 16)
                sp.dma_start(b1_sb[:], b1.rearrange("(k p) -> p k", p=P)).then_inc(s_w, 16)
                sp.dma_start(Wg_sb[:], Wg.rearrange("(k p) e -> p k e", p=P)).then_inc(s_w, 16)
                sp.dma_start(bg_sb[:], bg.partition_broadcast(P)).then_inc(s_w, 16)

            def load_x(G):
                if from_group(G, 2):
                    sp.wait_ge(s_mv, G.n - 1)
                sp.dma_start(x_all[:, bass.ds(G.n * Q, Q), 0:F],
                             x[bass.ds(G.n * GT, GT), :].rearrange("(t p) f -> p t f", p=P)
                             ).then_inc(s_x[G.p], 16)

            run_stages(sp, GROUPS, 2, 4, [(0, load_x)])

        @block.gpsimd
        def _(pool):
            pool.memset(bd_sb[:], 0.0).then_inc(s_bd, 1)
            pool.memset(ident[:], 1.0).then_inc(s_const, 1)
            pool.memset(mhalf[:], -0.5).then_inc(s_const, 1)
            pool.memset(ones[:], 1.0).then_inc(s_const, 1)
            pool.wait_ge(s_const, 1)
            pool.affine_select(out=ident[:], in_=ident[:], compare_op=ALU.is_equal, fill=0.0,
                               base=0, pattern=[[-1, P]], channel_multiplier=1).then_inc(s_const, 1)

            def rstd_of(G):
                wait_apart(pool, s_mv, G.n + 1, s_passed)
                pool.tensor_scalar(veps[G.p][:], mv[G.p][:, :, 1], EPS, None, ALU.add).then_inc(s_veps, 1)
                pool.wait_ge(s_veps, G.n + 1)
                pool.tensor_tensor(rstd[G.p][:], veps[G.p][:], mhalf[:], ALU.pow).then_inc(s_rstd, 1)

            def guard_args(G):
                wait_apart(pool, s_emax, G.n + 1, s_passed)
                pool.partition_all_reduce(guard[G.p][:].rearrange("p b h -> p (b h)"),
                                          emax[G.p][:].rearrange("p b h -> p (b h)"), P, MAX
                                          ).then_inc(s_guard, 1)
                pool.wait_ge(s_guard, G.n + 1)
                for b in range(GB):
                    g_b = guard[G.p][:, b:b + 1, :].broadcast_to([P, JT, H])
                    t_b = slice(b * JT, (b + 1) * JT)
                    pool.tensor_tensor(shifted[G.p][:, 0, t_b, :], eh[G.p][:, 0, t_b, :], g_b, ALU.subtract)
                    last = pool.tensor_tensor(shifted[G.p][:, 1, t_b, :], eh[G.p][:, 1, t_b, :], g_b, ALU.add)
                last.then_inc(s_shift, 1)
                wait_apart(pool, s_shift, G.n + 1, s_passed)
                pool.tensor_scalar(args[G.p][:, 0], shifted[G.p][:, 0], 1.0, SCALE_LN, ALU.mult, ALU.add)
                pool.tensor_scalar(args[G.p][:, 1], shifted[G.p][:, 0], 0.2, SCALE_LN, ALU.mult, ALU.add)
                pool.tensor_scalar(args[G.p][:, 2], shifted[G.p][:, 1], 0.0, -0.8, ALU.max, ALU.mult
                                   ).then_inc(s_args, 1)

            def V_low(G):
                pool.wait_ge(s_V, G.n + 1)
                pool.wait_ge(s_Vhi, G.n + 1)
                flat = "p q h t d -> p (q h t d)"
                pool.tensor_tensor(Vlo[G.p][:].rearrange(flat), V[G.p][:].rearrange(flat),
                                   Vhi[G.p][:].rearrange(flat), ALU.subtract).then_inc(s_Vlo, 1)

            def x_minus_1(G):
                if from_group(G, 2):
                    pool.wait_ge(s_x2, G.n - 1)
                pool.tensor_tensor(xm1[G.p][:], x_all[:, bass.ds(G.n * Q, Q), 0:F], ones[:], ALU.subtract
                                   ).then_inc(s_xm1, 1)

            def h_out(G):
                pool.wait_ge(s_rden, G.n + 1)
                pool.tensor_tensor(hh[G.p][:].rearrange("p q (h d) -> p (q h) d", h=H),
                                   num[G.p][:, :, :, 0:D].rearrange("p q h d -> p (q h) d"),
                                   rden[G.p][:].rearrange("p q h -> p (q h)").unsqueeze(2).broadcast_to([P, Q * H, D]),
                                   ALU.mult).then_inc(s_hh, 1)

            run_stages(pool, GROUPS, 2, START1, [
                (2, V_low), (0, rstd_of), (1, guard_args), (3, h_out), (3, x_minus_1)])

        @block.scalar
        def _(act):
            act.dma_start(W1_sb[:], W1[:, :]).then_inc(s_w, 16)
            for half in range(2):
                act.dma_start(Wd_sb[:, half * 16:(half + 1) * 16, :],
                              Wd[half * 4:(half + 1) * 4].rearrange("e (k p) c -> p (e k) c", p=P)
                              ).then_inc(s_w, 16)
            act.wait_ge(s_bd, 1)
            for part in (0, LO):
                act.dma_start(bd_sb[part:part + 1].rearrange("p k c -> p (k c)"),
                              bd.rearrange("(o e) c -> o (e c)", o=1)).then_inc(s_w, 16)

            def xT_out(G):
                act.wait_ge(s_xT, G.n + 1)
                if from_group(G, 2):
                    act.wait_ge(s_ei, H * (G.n - 1))
                act.activation(xTs[G.p][:], xT_ps[:], ACT.Copy).then_inc(s_xTs, 1)

            def exps(G):
                act.wait_ge(s_args, G.n + 1)
                if from_group(G, 2):
                    act.wait_ge(s_num, Q // 2 * (G.n - 1))
                act.activation(ex[G.p][:].rearrange("p t q h -> p (t q h)"),
                               args[G.p][:].rearrange("p t q h -> p (t q h)"), ACT.Exp).then_inc(s_ex, 1)

            def V_high(G):
                act.wait_ge(s_V, G.n + 1)
                if from_group(G, 2):
                    act.wait_ge(s_agg, Q * (G.n - 1))
                flat = "p q h t d -> p (q h t d)"
                act.activation(Vhi[G.p][:].rearrange(flat), V[G.p][:].rearrange(flat), ACT.Copy).then_inc(s_Vhi, 1)

            def exp_h(G):
                act.wait_ge(s_hh, G.n + 1)
                act.activation(eh_exp[G.p][:], hh[G.p][:], ACT.Exp).then_inc(s_eexp, 1)

            def steep_heads(heads):
                def body(G):
                    for h in heads:
                        act.wait_ge(s_ei, H * G.n + h + 1)
                        if h == 0:
                            act.wait_ge(s_eh, G.n + 1)
                        if from_group(G, 1) or h >= 2:
                            act.wait_ge(s_C, H * G.n + h - 1)
                        for b in range(GB):
                            for jt in range(JT):
                                last = act.activation(steep[h % 2][:, b, jt, :], ei_ps[h][:, b * N:(b + 1) * N],
                                                      ACT.Relu, bias=eh[G.p][:, 2, JT * b + jt, h:h + 1], scale=STEEP)
                        last.then_inc(s_steep, 1)
                return body

            run_stages(act, GROUPS, 2, START1, [
                (2, steep_heads((0,))), (1, xT_out), (2, V_high), (2, steep_heads((1,))), (4, exp_h),
                (2, steep_heads((2, 3))), (1, exps)])

        @block.tensor
        def _(pe):
            pe.wait_ge(s_const, 4)
            pe.wait_ge(s_adjf, 1)
            for jt in range(JT):
                for it in range(JT):
                    last = pe.transpose(setup_ps[:, jt * N + it * P:jt * N + (it + 1) * P],
                                        adj_f[:, it, jt * P:(jt + 1) * P], ident[:])
            last.then_inc(s_adjT, 1)

            def transposes(G):
                pe.wait_ge(s_xn, G.n + 1)
                if from_group(G, 1):
                    pe.wait_ge(s_xTs, G.n)
                for q in range(Q):
                    last = pe.transpose(xT_ps[:, q * P:(q + 1) * P], xn[G.p][:, q, :], ident[:])
                last.then_inc(s_xT, 1)

            def project(G):
                pe.wait_ge(s_xTs, G.n + 1)
                if not from_group(G, 1):
                    pe.wait_ge(s_wa, 4)
                else:
                    pe.wait_ge(s_V, G.n)
                for q in range(Q):
                    last = pe.matmul(Wh_ps[:, q, 0:F + 3 * H], xTs[G.p][:, q * P:(q + 1) * P],
                                     Wcat[:], start=True, stop=True)
                last.then_inc(s_wh, 1)

            def ei_heads(heads):
                def body(G):
                    for h in heads:
                        if h in (0, 2) and (from_group(G, 1) or h == 2):
                            pe.wait_ge(s_steep, H * G.n + h - 1)
                        if h in (1, 3) and from_group(G, 1):
                            pe.wait_ge(s_steep, H * (G.n - 1) + h + 1)
                        pe.matmul(ei_ps[h][:], Wa1rep[:, h, :], xTs[G.p][:], start=True, stop=True
                                  ).then_inc(s_ei, 1)
                return body

            def sum_tiles(tiles):
                def body(G):
                    if 0 in tiles:
                        pe.wait_ge(s_C, H * (G.n + 1))
                        pe.wait_ge(s_Vlo, G.n + 1)
                    for q in tiles:
                        if q % 2 == 0 and (from_group(G, 1) or q >= 2):
                            pe.wait_ge(s_num, Q // 2 * G.n + q // 2)
                        b, i_cols = q // JT, slice((q % JT) * P, (q % JT + 1) * P)
                        dst = agg_ps[:, q % 2]
                        parts = [(jt, v[G.p]) for jt in range(JT) for v in (Vhi, Vlo)]
                        for n, (jt, v) in enumerate(parts):
                            pe.matmul(dst[:, :, 1, :], negmask[:, jt, i_cols], v[:, JT * b + jt, :, 1, :],
                                      start=(n == 0), stop=False, skip_group_check=True)
                        for h in range(H):
                            for n, (jt, v) in enumerate(parts):
                                last = pe.matmul(dst[:, h, :, :].rearrange("p t d -> p (t d)"),
                                                 C[G.p][:, h, b, jt, i_cols],
                                                 v[:, JT * b + jt, h, :, :].rearrange("p t d -> p (t d)"),
                                                 start=False, stop=(h == H - 1 and n == 3),
                                                 skip_group_check=True)
                        last.then_inc(s_agg, 1)
                return body

            run_stages(pe, GROUPS, 2, START1, [
                (1, transposes), (3, sum_tiles((0, 1))), (2, ei_heads((2,))), (1, project), (2, ei_heads((3,))),
                (3, sum_tiles((2, 3))), (1, ei_heads((0, 1)))])

        @block.vector
        def _(dve):
            dve.wait_ge(s_adj, 16)
            dve.tensor_scalar(adj_f[:], adj_i[:], 0.0, None, ALU.is_gt).then_inc(s_adjf, 1)
            dve.wait_ge(s_w, 16 * WLOADS)
            Wv = Wcat[:, 0:F].rearrange("p (h d) -> p h d", h=H)
            for half in range(2):
                last = dve.tensor_tensor(wa_prod[:, half], Wv, a_sb[:, :, 1 - half, :], ALU.mult)
            last.then_inc(s_wa, 1)
            dve.wait_ge(s_wa, 1)
            dve.tensor_reduce(Wcat[:, F:F + 2 * H].rearrange("p (t h) -> p t h", t=2), wa_prod[:],
                              AX.X, ALU.add).then_inc(s_wa, 1)
            dve.wait_ge(s_wa, 2)
            dve.tensor_scalar(Wcat[:, F + 2 * H:], Wcat[:, F:F + H], STEEP, None, ALU.mult).then_inc(s_wa, 1)
            dve.tensor_copy(Wa1rep[:], Wcat[:, F + H:F + 2 * H].unsqueeze(2).broadcast_to([P, H, P])
                            ).then_inc(s_wa, 1)
            dve.wait_ge(s_adjT, 1)
            flat = "p t i -> p (t i)"
            dve.tensor_copy(mask[:].rearrange(flat), setup_ps[:])
            dve.tensor_scalar(negmask[:].rearrange(flat), setup_ps[:], -1.0, None, ALU.mult).then_inc(s_mask, 1)
            dve.wait_ge(s_mask, 1)
            dve.tensor_scalar(W1_hi[:], W1_sb[:], W_SCALE, None, ALU.mult).then_inc(s_mask, 1)
            dve.wait_ge(s_mask, 2)
            dve.scalar_tensor_tensor(W1_lo[:], W1_sb[:], W_SCALE, W1_hi[:], ALU.mult, ALU.subtract
                                     ).then_inc(s_mask, 1)

            def stats_of(G):
                dve.wait_ge(s_x[G.p], 16 * (G.k + 1))
                for q in range(Q):
                    last = dve.bn_stats(stats[G.p][:, q, :], x_all[:, bass.ds(G.n * Q + q, 1), 0:F].rearrange("p q f -> p (q f)"))
                last.then_inc(s_bn, 1)
                wait_apart(dve, s_bn, G.n + 1, s_passed)
                for q in range(Q):
                    last = dve.bn_aggr(mv[G.p][:, q, :], stats[G.p][:, q, :])
                last.then_inc(s_mv, 1)

            def normalise(G):
                dve.wait_ge(s_rstd, G.n + 1)
                if from_group(G, 2):
                    dve.wait_ge(s_xT, G.n - 1)
                for q in range(Q):
                    last = dve.tensor_scalar(xn[G.p][:, q, :], x_all[:, bass.ds(G.n * Q + q, 1), 0:F].rearrange("p q f -> p (q f)"),
                                             mv[G.p][:, q, 0:1], rstd[G.p][:, q:q + 1], ALU.subtract, ALU.mult)
                last.then_inc(s_xn, 1)

            def e_out(G):
                dve.wait_ge(s_wh, G.n + 1)
                dve.tensor_copy(eh[G.p][:], Wh_ps[:, :, F:F + 3 * H].rearrange("p q (t h) -> p t q h", t=3)
                                ).then_inc(s_eh, 1)
                dve.wait_ge(s_eh, G.n + 1)
                ev = eh[G.p][:, 0].rearrange("p (b t) h -> p t b h", b=GB)
                dve.tensor_tensor(emax[G.p][:], ev[:, 0], ev[:, 1], ALU.max).then_inc(s_emax, 1)

            def C_heads(heads):
                def body(G):
                    if 0 in heads and from_group(G, 2):
                        dve.wait_ge(s_agg, Q * (G.n - 1))
                    for h in heads:
                        dve.wait_ge(s_steep, H * G.n + h + 1)
                        dve.tensor_tensor(C[G.p][:, h].rearrange("p b t i -> p b (t i)"),
                                          steep[h % 2][:].rearrange("p b t i -> p b (t i)"),
                                          mask[:].rearrange("p t i -> p (t i)").unsqueeze(1).broadcast_to([P, GB, JT * N]),
                                          ALU.min).then_inc(s_C, 1)
                return body

            def V_out(G):
                dve.wait_ge(s_ex, G.n + 1)
                Wh = Wh_ps[:, :, 0:F].rearrange("p q (h d) -> p q h d", h=H)
                for t in range(2):
                    dve.tensor_tensor(V[G.p][:, :, :, t, 0:D], Wh,
                                      ex[G.p][:, t].unsqueeze(3).broadcast_to([P, Q, H, D]), ALU.mult)
                dve.tensor_copy(V[G.p][:, :, :, :, D], ex[G.p][:, 0:2].rearrange("p t q h -> p q h t")
                                ).then_inc(s_V, 1)

            def divide(half):
                def body(G):
                    two = slice(2 * half, 2 * half + 2)
                    dve.wait_ge(s_agg, Q * G.n + 2 * half + 2)
                    if half == 0 and from_group(G, 2):
                        dve.wait_ge(s_hh, G.n - 1)
                    dve.tensor_tensor(rB[:, two], agg_ps[:, :, :, 1, :],
                                      ex[G.p][:, 2, two, :].unsqueeze(3).broadcast_to([P, 2, H, D1]), ALU.mult
                                      ).then_inc(s_rB, 1)
                    dve.wait_ge(s_rB, Q // 2 * G.n + half + 1)
                    dve.tensor_tensor(num[G.p][:, two], agg_ps[:, :, :, 0, :], rB[:, two], ALU.subtract
                                      ).then_inc(s_num, 1)
                return body

            def invert(G):
                dve.wait_ge(s_num, Q // 2 * (G.n + 1))
                dve.reciprocal(rden[G.p][:], num[G.p][:, :, :, D]).then_inc(s_rden, 1)

            def add_elu(G):
                if from_group(G, 1):
                    dve.wait_ge(s_x2, G.n)
                dve.wait_ge(s_xm1, G.n + 1)
                dve.wait_ge(s_hh, G.n + 1)
                dve.scalar_tensor_tensor(x_relu[:], hh[G.p][:], 0.0, xm1[G.p][:], ALU.max, ALU.add
                                         ).then_inc(s_relu, 1)
                dve.wait_ge(s_relu, G.n + 1)
                dve.wait_ge(s_eexp, G.n + 1)
                dve.scalar_tensor_tensor(x_all[:, bass.ds(G.n * Q, Q), 0:F], eh_exp[G.p][:], 1.0, x_relu[:],
                                         ALU.min, ALU.add).then_inc(s_x2, 1)

            run_stages(dve, GROUPS, 2, START1, [
                (2, V_out), (2, C_heads((0,))), (0, stats_of), (3, divide(0)), (2, C_heads((1,))),
                (1, e_out), (3, divide(1)), (3, invert), (2, C_heads((2,))), (0, normalise), (4, add_elu),
                (2, C_heads((3,)))])

        block1.__exit__(None, None, None)
        phase1.close()

        H_sb = [sb(f"H{i}", [P, KC, GT]) for i in range(3)]
        h_ps = bank[1:5]
        gate_ps = bank[5]
        rank_ps = bank[6]
        total_ps = bank[7]
        xT_hi = [sb(f"xT_hi{i}", [P, GT], F16) for i in range(3)]
        xT_lo = [sb(f"xT_lo{i}", [P, GT], F16) for i in range(3)]
        iota_e = sb("iota_e", [P, E])
        base_e = sb("base_e", [P, E])
        before = sb("before", [P, P], F16)
        ones16 = sb("ones16", [P, P], F16)
        meta = sb("meta", [P, TILES, 4])
        lg = sb("lg", [P, Q, E])
        top = sb("top", [P, Q])
        below = [sb(f"below{i}", [P, Q, E]) for i in range(2)]
        cand = sb("cand", [P, Q, E])
        first = sb("first", [P, Q])
        hot = [sb(f"hot{i}", [P, Q, E], F16) for i in range(2)]
        hot_all = sb("hot_all", [P, E], F16)
        hot_sum = [sb(f"hot_sum{i}", [P, E], F16) for i in range(2)]
        half_tanh = [sb(f"half_tanh{i}", [P, Q, E]) for i in range(2)]
        less = sb("less", [P, Q, E])
        part = sb("part", [P, Q, E])
        total = sb("total", [P, Q])
        total_exp = sb("total_exp", [P, Q])
        ranked = sb("ranked", [P, Q, E])
        masked = sb("masked", [P, Q, E])
        place = [sb(f"place{i}", [P, Q], U32) for i in range(2)]
        place_f = sb("place_f", [P, Q])
        rows = [sb(f"rows{i}", [P, Q, ROW]) for i in range(2)]
        nobody = sb("nobody", [P, ROW])

        s2_const = sem("p2_constants")
        s2_bn = sem("p2_stats_of_tiles")
        s2_mv = sem("p2_mean_var_ready")
        s2_veps = sem("p2_var_eps")
        s2_rstd = sem("p2_rstd_ready")
        s2_meta = sem("p2_meta_kept")
        s2_xn = sem("p2_normalised")
        s2_xT = sem("p2_transposed")
        s2_hi = sem("p2_high_part")
        s2_lo = sem("p2_low_part")
        s2_h = sem("p2_hidden_chunks")
        s2_gelu = sem("p2_gelu_chunks")
        s2_gate = sem("p2_gate_logits")
        s2_top = sem("p2_top_chain")
        s2_below = sem("p2_logits_below_top")
        s2_hot = sem("p2_onehot_ready")
        s2_sum = sem("p2_onehot_sums")
        s2_tanh = sem("p2_tanh_ready")
        s2_gate_step = sem("p2_gate_chain")
        s2_rank = sem("p2_ranks_ready")
        s2_ranked = sem("p2_ranks_chain")
        s2_place = sem("p2_places_ready")
        s2_x = sem("p2_x_in_rows")
        s2_rows = sem("p2_rows_ready")
        s2_put = [sem("p2_rows_stored0"), sem("p2_rows_stored1")]
        s2_nobody = sem("p2_nobody_stored")
        s2_hot_all = sem("p2_onehots_of_group_summed")
        s2_wd = sem("p2_expert_weights_split")
        START2 = 6

        with nc.Block() as block:
            @block.sync
            def _(sp):
                sp.wait_ge(s2_const, 8)
                sp.dma_start(lists[E * LIST:E * LIST + P, :], nobody[:]).then_inc(s2_nobody, 16)
                sp.wait_ge(s2_nobody, 16)

            @block.gpsimd
            def _(pool):
                pool.memset(nobody[:], 0.0).then_inc(s2_const, 1)
                pool.memset(ones16[:], 1.0).then_inc(s2_const, 1)
                pool.memset(hot_sum[0][:], 0.0).then_inc(s2_const, 1)
                pool.iota(iota_e[:], pattern=[[1, E]], base=-E, channel_multiplier=0,
                          allow_small_or_imprecise_dtypes=True).then_inc(s2_const, 1)
                pool.iota(base_e[:], pattern=[[LIST, E]], base=0, channel_multiplier=0,
                          allow_small_or_imprecise_dtypes=True).then_inc(s2_const, 1)
                pool.iota(meta[:, :, 3], pattern=[[P, TILES]], base=0, channel_multiplier=1,
                          allow_small_or_imprecise_dtypes=True).then_inc(s2_const, 1)
                pool.wait_ge(s2_const, 6)
                pool.memset(nobody[:, ROW - 1:ROW], float(NOBODY)).then_inc(s2_const, 1)
                pool.affine_select(out=before[:], in_=ones16[:], compare_op=ALU.is_gt, fill=0.0, base=0,
                                   pattern=[[1, P]], channel_multiplier=-1).then_inc(s2_const, 1)

                def rstd_of(G):
                    wait_apart(pool, s2_mv, G.n + 1, s_passed)
                    pool.tensor_scalar(veps[G.p][:], mv[G.p][:, :, 1], EPS, None, ALU.add).then_inc(s2_veps, 1)
                    pool.wait_ge(s2_veps, G.n + 1)
                    pool.tensor_tensor(mv[G.p][:, :, 1], veps[G.p][:], mhalf[:], ALU.pow).then_inc(s2_rstd, 1)
                    pool.wait_ge(s2_rstd, G.n + 1)
                    pool.tensor_copy(meta[:, bass.ds(G.n * Q, Q), 0:2], mv[G.p][:]).then_inc(s2_meta, 1)

                def put(G):
                    pool.wait_ge(s2_place, G.n + 1)
                    pool.tensor_copy(rows[G.p][:, :, F:ROW], meta[:, bass.ds(G.n * Q, Q), :]).then_inc(s2_rows, 1)
                    wait_apart(pool, s2_x, G.n + 1, s_passed)
                    wait_apart(pool, s2_rows, G.n + 1, s_passed)
                    for q in range(Q):
                        pool.indirect_dma_start(
                            out=lists[:, :], out_offset=bass.IndirectOffsetOnAxis(ap=place[G.p][:, q:q + 1], axis=0),
                            in_=rows[G.p][:, q, :], in_offset=None).then_inc(s2_put[G.p], 16)

                run_stages(pool, GROUPS, 2, START2, [(0, rstd_of), (4, put)])
                for i in range(2):
                    pool.wait_ge(s2_put[i], 16 * Q * GROUPS // 2)

            @block.scalar
            def _(act):
                def high_part(G):
                    act.wait_ge(s2_xT, G.n + 1)
                    if from_group(G, 2):
                        act.wait_ge(s2_h, KC * (G.n - 1))
                    act.activation(xT_hi[G.p][:], xT_ps[:], ACT.Copy).then_inc(s2_hi, 1)

                def gelu(G):
                    if from_group(G, 2):
                        act.wait_ge(s2_gate, G.n - 1)
                    for k in range(KC):
                        act.wait_ge(s2_h, KC * G.n + k + 1)
                        act.activation(H_sb[G.p][:, k, :], h_ps[k][:], ACT.Gelu, bias=b1_sb[:, k:k + 1],
                                       scale=1.0 / W_SCALE).then_inc(s2_gelu, 1)

                def tanh(G):
                    act.wait_ge(s2_below, G.n + 1)
                    if from_group(G, 2):
                        act.wait_ge(s2_gate_step, 4 * (G.n - 1))
                    act.activation(half_tanh[G.p][:], below[G.p][:], ACT.Tanh, scale=0.5).then_inc(s2_tanh, 1)

                def x_in_rows(G):
                    if from_group(G, 2):
                        act.wait_ge(s2_put[G.p], 16 * Q * G.k)
                    act.activation(rows[G.p][:, :, 0:F], x_all[:, bass.ds(G.n * Q, Q), :], ACT.Copy).then_inc(s2_x, 1)

                for part8 in range(4):
                    c = slice(part8 * KC * 2, (part8 + 1) * KC * 2)
                    act.activation(Wd_hi[:, c, :], Wd_sb[:, c, :], ACT.Copy, scale=W_SCALE)
                act.activation(bd2[:], bd_sb[:], ACT.Copy, scale=W_SCALE).then_inc(s2_wd, 1)
                run_stages(act, GROUPS, 2, START2, [(4, tanh), (2, gelu), (1, high_part), (4, x_in_rows)])

            @block.tensor
            def _(pe):
                def transposes(G):
                    pe.wait_ge(s2_xn, G.n + 1)
                    if from_group(G, 1):
                        pe.wait_ge(s2_lo, G.n)
                    for q in range(Q):
                        last = pe.transpose(xT_ps[:, q * P:(q + 1) * P], xn[G.p][:, q, :], ident[:])
                    last.then_inc(s2_xT, 1)

                def hidden(G):
                    pe.wait_ge(s2_lo, G.n + 1)
                    for k in range(KC):
                        cols = slice(k * P, (k + 1) * P)
                        if from_group(G, 1):
                            pe.wait_ge(s2_gelu, KC * (G.n - 1) + k + 1)
                        pe.matmul(h_ps[k][:], W1_hi[:, cols], xT_lo[G.p][:], start=True, stop=False)
                        pe.matmul(h_ps[k][:], W1_lo[:, cols], xT_hi[G.p][:], start=False, stop=False)
                        pe.matmul(h_ps[k][:], W1_hi[:, cols], xT_hi[G.p][:], start=False, stop=True).then_inc(s2_h, 1)

                def gate(G):
                    pe.wait_ge(s2_gelu, KC * (G.n + 1))
                    if from_group(G, 1):
                        pe.wait_ge(s2_top, 4 * (G.n - 1) + 1)
                    for q in range(Q):
                        for k in range(KC):
                            last = pe.matmul(gate_ps[:, q * E:(q + 1) * E], H_sb[G.p][:, k, q * P:(q + 1) * P],
                                             Wg_sb[:, k, :], start=(k == 0), stop=(k == KC - 1))
                    last.then_inc(s2_gate, 1)

                def rank(G):
                    pe.wait_ge(s2_hot, G.n + 1)
                    if from_group(G, 1):
                        pe.wait_ge(s2_ranked, 3 * (G.n - 1) + 1)
                    flat = "p q e -> p (q e)"
                    pe.matmul(rank_ps[:, 0:Q * E], before[:], hot[G.p][:].rearrange(flat), start=True, stop=False,
                              skip_group_check=True)
                    for q in range(Q - 1):
                        pe.matmul(rank_ps[:, (q + 1) * E:Q * E], ones16[:],
                                  hot[G.p][:, q:q + 1, :].broadcast_to([P, Q - 1 - q, E]), start=False, stop=False,
                                  skip_group_check=True)
                    if from_group(G, 1):
                        pe.wait_ge(s2_sum, G.n)
                    pe.matmul(rank_ps[:, 0:Q * E], ones16[:], hot_sum[G.p][:].unsqueeze(1).broadcast_to([P, Q, E]),
                              start=False, stop=True, skip_group_check=True).then_inc(s2_rank, 1)

                pe.wait_ge(s2_const, 8)
                run_stages(pe, GROUPS, 2, START2, [(2, hidden), (1, transposes), (4, rank), (3, gate)])
                pe.wait_ge(s2_sum, GROUPS)
                pe.matmul(total_ps[:, 0:E], ones16[:], hot_sum[GROUPS % 2][:], start=True, stop=True)

            @block.vector
            def _(dve):
                def stats_of(G):
                    if from_group(G, 2):
                        dve.wait_ge(s2_meta, G.n - 1)
                    for q in range(Q):
                        last = dve.bn_stats(stats[G.p][:, q, :],
                                            x_all[:, bass.ds(G.n * Q + q, 1), :].rearrange("p q f -> p (q f)"))
                    last.then_inc(s2_bn, 1)
                    wait_apart(dve, s2_bn, G.n + 1, s_passed)
                    for q in range(Q):
                        last = dve.bn_aggr(mv[G.p][:, q, :], stats[G.p][:, q, :])
                    last.then_inc(s2_mv, 1)

                def normalise(G):
                    dve.wait_ge(s2_rstd, G.n + 1)
                    if from_group(G, 2):
                        dve.wait_ge(s2_xT, G.n - 1)
                    for q in range(Q):
                        last = dve.tensor_scalar(xn[G.p][:, q, :],
                                                 x_all[:, bass.ds(G.n * Q + q, 1), :].rearrange("p q f -> p (q f)"),
                                                 mv[G.p][:, q, 0:1], mv[G.p][:, q, 1:2], ALU.subtract, ALU.mult)
                    last.then_inc(s2_xn, 1)

                def low_part(G):
                    dve.wait_ge(s2_hi, G.n + 1)
                    dve.tensor_tensor(xT_lo[G.p][:], xT_ps[:], xT_hi[G.p][:], ALU.subtract).then_inc(s2_lo, 1)

                def over_e(ap):
                    return ap.unsqueeze(2).broadcast_to([P, Q, E])

                def over_q(ap):
                    return ap.unsqueeze(1).broadcast_to([P, Q, E])

                def choose(G):
                    base = 4 * G.n
                    dve.wait_ge(s2_gate, G.n + 1)
                    dve.tensor_tensor(lg[:], gate_ps[:, 0:Q * E].rearrange("p (q e) -> p q e", q=Q),
                                      over_q(bg_sb[:]), ALU.add).then_inc(s2_top, 1)
                    dve.wait_ge(s2_top, base + 1)
                    dve.tensor_reduce(top[:], lg[:], AX.X, ALU.max).then_inc(s2_top, 1)
                    dve.wait_ge(s2_top, base + 2)
                    if from_group(G, 2):
                        dve.wait_ge(s2_tanh, G.n - 1)
                    dve.tensor_tensor(below[G.p][:], lg[:], over_e(top[:]), ALU.subtract).then_inc(s2_below, 1)
                    dve.wait_ge(s2_below, G.n + 1)
                    dve.scalar_tensor_tensor(cand[:], below[G.p][:], 0.0, over_q(iota_e[:]), ALU.is_equal, ALU.mult
                                             ).then_inc(s2_top, 1)

                def one_hot(G):
                    dve.wait_ge(s2_top, 4 * G.n + 3)
                    dve.tensor_reduce(first[:], cand[:], AX.X, ALU.min).then_inc(s2_top, 1)
                    dve.wait_ge(s2_top, 4 * G.n + 4)
                    if from_group(G, 2):
                        dve.wait_ge(s2_rank, G.n - 1)
                    dve.tensor_tensor(hot[G.p][:], over_q(iota_e[:]), over_e(first[:]), ALU.is_equal).then_inc(s2_hot, 1)

                def sum_up(G):
                    dve.wait_ge(s2_hot, G.n + 1)
                    if from_group(G, 1):
                        dve.wait_ge(s2_sum, G.n)
                    with nc.allow_low_precision("counts up to the number of tiles"):
                        dve.tensor_reduce(hot_all[:], hot[G.p][:].rearrange("p q e -> p e q"), AX.X, ALU.add
                                          ).then_inc(s2_hot_all, 1)
                    dve.wait_ge(s2_hot_all, G.n + 1)
                    if from_group(G, 1):
                        dve.wait_ge(s2_rank, G.n)
                    dve.tensor_tensor(hot_sum[1 - G.p][:], hot_sum[G.p][:], hot_all[:], ALU.add).then_inc(s2_sum, 1)

                def places(G):
                    chain, gates = 3 * G.n, 4 * G.n
                    dve.wait_ge(s2_rank, G.n + 1)
                    dve.tensor_tensor(ranked[:], rank_ps[:, 0:Q * E].rearrange("p (q e) -> p q e", q=Q),
                                      over_q(base_e[:]), ALU.add).then_inc(s2_ranked, 1)
                    dve.wait_ge(s2_tanh, G.n + 1)
                    dve.tensor_scalar(less[:], half_tanh[G.p][:], -1.0, 1.0, ALU.mult, ALU.add).then_inc(s2_gate_step, 1)
                    dve.wait_ge(s2_ranked, chain + 1)
                    dve.tensor_tensor(masked[:], ranked[:], hot[G.p][:], ALU.mult).then_inc(s2_ranked, 1)
                    dve.wait_ge(s2_gate_step, gates + 1)
                    dve.reciprocal(part[:], less[:]).then_inc(s2_gate_step, 1)
                    dve.wait_ge(s2_ranked, chain + 2)
                    dve.tensor_reduce(place_f[:], masked[:], AX.X, ALU.add).then_inc(s2_ranked, 1)
                    dve.wait_ge(s2_gate_step, gates + 2)
                    dve.tensor_reduce(total[:], part[:], AX.X, ALU.add).then_inc(s2_gate_step, 1)
                    dve.wait_ge(s2_ranked, chain + 3)
                    if from_group(G, 2):
                        dve.wait_ge(s2_put[G.p], 16 * Q * G.k)
                    dve.tensor_copy(place[G.p][:], place_f[:])
                    dve.wait_ge(s2_gate_step, gates + 3)
                    dve.tensor_scalar(total_exp[:], total[:], 2.0 * W_SCALE, -E * W_SCALE, ALU.mult, ALU.add).then_inc(s2_gate_step, 1)
                    dve.wait_ge(s2_gate_step, gates + 4)
                    dve.reciprocal(meta[:, bass.ds(G.n * Q, Q), 2], total_exp[:]).then_inc(s2_place, 1)

                dve.wait_ge(s2_const, 8)
                run_stages(dve, GROUPS, 2, START2, [
                    (4, choose), (4, one_hot), (1, normalise), (0, stats_of), (4, places), (1, low_part),
                    (4, sum_up)])
                dve.wait_ge(s2_wd, 1)
                for part8 in range(4):
                    c = slice(part8 * KC * 2, (part8 + 1) * KC * 2)
                    dve.scalar_tensor_tensor(Wd_lo[:, c, :], Wd_sb[:, c, :], W_SCALE, Wd_hi[:, c, :],
                                             ALU.mult, ALU.subtract)
                dve.scalar_tensor_tensor(bd2[LO:LO + 1], bd_sb[LO:LO + 1], W_SCALE, bd2[LO:LO + 1],
                                         ALU.mult, ALU.subtract).then_inc(s2_wd, 1)
                dve.wait_ge(s2_wd, 2)

        slot_f = sb("slot_f", [1, SLOTS])
        count = sb("count", [1, E])
        count_i = sb("count_i", [1, E], I32)
        blocks_i = sb("blocks_i", [1, E], I32)
        blocks_f = sb("blocks_f", [1, E])
        cum = [sb(f"cum{i}", [1, E]) for i in range(2)]
        room = sb("room", [1, E])
        tail_f = sb("tail_f", [1, E])
        tail_i = sb("tail_i", [1, E], I32)
        past = sb("past", [1, SLOTS, E])
        jumps = sb("jumps", [1, SLOTS, E])
        expert_f = sb("expert_f", [1, SLOTS])
        expert_i = sb("expert_i", [1, SLOTS], I32)
        start_f = sb("start_f", [1, SLOTS])
        start_i = sb("start_i", [1, SLOTS], I32)

        s3_const = sem("p3_constants")
        s3 = sem("p3_vector_step")
        s3_tail = sem("p3_tails_ready")
        s3_fill = sem("p3_tails_stored")

        with nc.Block() as block:
            @block.gpsimd
            def _(pool):
                pool.iota(slot_f[:], pattern=[[P, SLOTS]], base=0, channel_multiplier=0,
                          allow_small_or_imprecise_dtypes=True).then_inc(s3_const, 1)

            def fill(eng, experts):
                eng.wait_ge(s3_tail, 1)
                for e in experts:
                    tail = eng.value_load(tail_i[0:1, e:e + 1], min_val=0, max_val=E * LIST - P)
                    eng.dma_start(lists[bass.ds(tail, P), :], nobody[:]).then_inc(s3_fill, 16)
                eng.wait_ge(s3_fill, 16 * E)

            @block.sync
            def _(sp):
                fill(sp, range(0, E, 2))

            @block.scalar
            def _(act):
                fill(act, range(1, E, 2))

            @block.vector
            def _(dve):
                steps = [0]

                def step(instruction):
                    steps[0] += 1
                    instruction.then_inc(s3, 1)
                    dve.wait_ge(s3, steps[0])

                step(dve.tensor_copy(count[:], total_ps[0:1, 0:E]))
                step(dve.tensor_tensor(tail_f[:], count[:], base_e[0:1, :], ALU.add))
                dve.tensor_copy(tail_i[:], tail_f[:]).then_inc(s3_tail, 1)
                step(dve.tensor_scalar(count_i[:], count[:], float(P - 1), None, ALU.add))
                step(dve.tensor_scalar(blocks_i[:], count_i[:], P.bit_length() - 1, None, ALU.arith_shift_right))
                step(dve.tensor_scalar(blocks_f[:], blocks_i[:], float(P), None, ALU.mult))
                step(dve.tensor_scalar(room[:], blocks_f[0:1, :], -1.0, float(LIST), ALU.mult, ALU.add))
                step(dve.tensor_copy(cum[0][:], blocks_f[:]))
                n = 0
                for shift in (1, 2, 4):
                    dve.tensor_copy(cum[1 - n][:, 0:shift], cum[n][:, 0:shift])
                    step(dve.tensor_tensor(cum[1 - n][:, shift:], cum[n][:, shift:], cum[n][:, 0:E - shift], ALU.add))
                    n = 1 - n
                dve.wait_ge(s3_const, 1)
                step(dve.tensor_tensor(past[:], cum[n][0:1, :].unsqueeze(1).broadcast_to([1, SLOTS, E]),
                                       slot_f[:].unsqueeze(2).broadcast_to([1, SLOTS, E]), ALU.is_le))
                dve.tensor_reduce(expert_f[:], past[:], AX.X, ALU.add)
                step(dve.tensor_tensor(jumps[:], past[:], room[:].unsqueeze(1).broadcast_to([1, SLOTS, E]), ALU.mult))
                step(dve.tensor_reduce(start_f[:], jumps[:], AX.X, ALU.add))
                step(dve.tensor_tensor(start_f[:], start_f[:], slot_f[:], ALU.add))
                step(dve.tensor_scalar(start_i[:], start_f[:], float(E * LIST), None, ALU.min))
                dve.tensor_scalar(expert_i[:], expert_f[:], float(E - 1), float(KC), ALU.min, ALU.mult)

        NB4 = 3
        idx_out = [sb(f"idx_out{i}", [P, Q], U32) for i in range(NB4)]
        xg = [sb(f"xg{i}", [P, Q, ROW]) for i in range(NB4)]
        xn4 = [sb(f"xn4_{i}", [P, Q, F]) for i in range(NB4)]
        H_hi = [sb(f"H_hi{i}", [P, KC, GT], F16) for i in range(NB4)]
        H_lo = [sb(f"H_lo{i}", [P, KC, GT], F16) for i in range(NB4)]
        yo = [sb(f"yo{i}", [P, Q, F]) for i in range(NB4)]
        y_ps = bank[5:8]
        s4_in = [[sem(f"p4_rows_loaded{i}_{q}") for q in range(Q)] for i in range(NB4)]
        s4_xn = sem("p4_normalised")
        s4_xT = sem("p4_transposed")
        s4_hi = sem("p4_high_part")
        s4_lo = sem("p4_low_part")
        s4_h = sem("p4_hidden_chunks")
        s4_gelu = sem("p4_gelu_chunks")
        s4_Hhi = sem("p4_H_high_chunks")
        s4_Hlo = sem("p4_H_low_chunks")
        s4_Hlo_pool = sem("p4_H_last_low_chunk")
        s4_y = sem("p4_expert_tiles")
        s4_yo = sem("p4_rows_ready")
        s4_out = [sem(f"p4_rows_stored{i}") for i in range(NB4)]
        START4 = 6

        def values_of(eng, table, G, largest):
            return nc.values_load_multi_w_load_instructions(
                table[0:1, bass.ds(G.n * Q, Q)], engines=[eng.engine], min_val=0, max_val=largest)[1]

        with nc.Block() as block:
            @block.sync
            def _(sp):
                def load(G):
                    starts = values_of(sp, start_i, G, E * LIST)
                    for q in range(Q):
                        if from_group(G, 3):
                            sp.wait_ge(s4_yo, Q * (G.n - 3) + q + 1)
                        sp.dma_start(xg[G.p][:, q, :], lists[bass.ds(starts[q], P), :]).then_inc(s4_in[G.p][q], 16)

                run_stages(sp, SGROUPS, NB4, START4, [(0, load)])

            @block.gpsimd
            def _(pool):
                def H_low(G):
                    wait_apart(pool, s4_Hhi, KC * G.n + 1, s_passed)
                    if from_group(G, 3):
                        wait_apart(pool, s4_y, Q * (G.n - 2), s_passed)
                    pool.tensor_tensor(H_lo[G.p][:, 0, :], H_sb[G.p][:, 0, :], H_hi[G.p][:, 0, :],
                                       ALU.subtract).then_inc(s4_Hlo_pool, 1)

                def scatter(G):
                    wait_apart(pool, s4_yo, Q * (G.n + 1), s_passed)
                    for q in range(Q):
                        pool.indirect_dma_start(
                            out=out[:, :], out_offset=bass.IndirectOffsetOnAxis(ap=idx_out[G.p][:, q:q + 1], axis=0),
                            in_=yo[G.p][:, q, :], in_offset=None, bounds_check=B * N - 1, oob_is_err=False
                        ).then_inc(s4_out[G.p], 16)

                run_stages(pool, SGROUPS, NB4, START4, [(2, H_low), (3, scatter)])
                for i in range(NB4):
                    pool.wait_ge(s4_out[i], 16 * Q * SGROUPS // NB4)

            @block.scalar
            def _(act):
                def high_part(G):
                    act.wait_ge(s4_xT, G.n + 1)
                    if from_group(G, 3):
                        act.wait_ge(s4_h, KC * (G.n - 2))
                    act.activation(xT_hi[G.p][:], xT_ps[:], ACT.Copy).then_inc(s4_hi, 1)

                def gelu(k):
                    def body(G):
                        if k == 0 and from_group(G, 3):
                            act.wait_ge(s4_y, Q * (G.n - 2))
                        act.wait_ge(s4_h, KC * G.n + k + 1)
                        act.activation(H_sb[G.p][:, k, :], h_ps[k][:], ACT.Gelu, bias=b1_sb[:, k:k + 1],
                                       scale=1.0 / W_SCALE).then_inc(s4_gelu, 1)
                    return body

                def H_high(k):
                    def body(G):
                        act.wait_ge(s4_gelu, KC * G.n + k + 1)
                        act.activation(H_hi[G.p][:, k, :], H_sb[G.p][:, k, :], ACT.Copy).then_inc(s4_Hhi, 1)
                    return body

                run_stages(act, SGROUPS, NB4, START4, [
                    (2, gelu(0)), (2, gelu(1)), (2, H_high(0)), (2, H_high(1)), (2, gelu(2)), (1, high_part),
                    (2, H_high(2)), (2, gelu(3)), (2, H_high(3))])

            @block.tensor
            def _(pe):
                def transposes(G):
                    pe.wait_ge(s4_xn, G.n + 1)
                    if from_group(G, 1):
                        pe.wait_ge(s4_lo, G.n)
                    for q in range(Q):
                        last = pe.transpose(xT_ps[:, q * P:(q + 1) * P], xn4[G.p][:, q, :], ident[:])
                    last.then_inc(s4_xT, 1)

                def hidden(k, part):
                    W_part, x_part = ((W1_hi, xT_lo), (W1_lo, xT_hi), (W1_hi, xT_hi))[part]

                    def body(G):
                        if k == 0 and part == 0:
                            pe.wait_ge(s4_lo, G.n + 1)
                        if part == 0 and from_group(G, 1):
                            pe.wait_ge(s4_gelu, KC * (G.n - 1) + k + 1)
                        last = pe.matmul(h_ps[k][:], W_part[:, k * P:(k + 1) * P], x_part[G.p][:],
                                         start=(part == 0), stop=(part == 2))
                        if part == 2:
                            last.then_inc(s4_h, 1)
                    return body

                chosen = [None] * Q

                def load_experts(G):
                    chosen[:] = values_of(pe, expert_i, G, (E - 1) * KC)

                def expert(q, k):
                    def body(G):
                        if q == 0 and k == 0:
                            pe.wait_ge(s4_Hlo, 3 * (G.n + 1))
                            pe.wait_ge(s4_Hlo_pool, G.n + 1)
                        y = y_ps[(G.p + q) % NB4][:, 0:F]
                        if k == 0 and (from_group(G, 1) or q >= NB4):
                            pe.wait_ge(s4_yo, Q * G.n + q + 1 - NB4)
                        tile = (slice(None), k, slice(q * P, (q + 1) * P))
                        W_low = Wd_lo[:, bass.ds(chosen[q], KC), :][:, k, :]
                        W_high = Wd_hi[:, bass.ds(chosen[q], KC), :][:, k, :]
                        pe.matmul(y, H_hi[G.p][tile], W_low, start=(k == 0), stop=False)
                        pe.matmul(y, H_hi[G.p][tile], W_high, start=False, stop=False)
                        pe.matmul(y, H_lo[G.p][tile], W_high, start=False, stop=False)
                        if k == KC - 1:
                            bias = bd2[:, bass.ds(chosen[q], KC), :].rearrange("p k c -> p (k c)")
                            pe.matmul(y, ones16[0:LO + 1, :], bias, start=False, stop=True).then_inc(s4_y, 1)
                    return body

                def two_tiles(q0, k_hidden):
                    work = [(3, expert(q0 + n // KC, n % KC)) for n in range(2 * KC)]
                    for part, n in ((2, 6), (1, 3), (0, 0)):
                        work.insert(n, (2, hidden(k_hidden, part)))
                    return work

                first = [(2, hidden(k, part)) for k in range(2) for part in range(3)]
                run_stages(pe, SGROUPS, NB4, START4,
                           first + [(3, load_experts)] + two_tiles(0, 2) + [(1, transposes)] + two_tiles(2, 3))

            @block.vector
            def _(dve):
                def normalise(G):
                    if from_group(G, 3):
                        dve.wait_ge(s4_xT, G.n - 2)
                    for q in range(Q):
                        dve.wait_ge(s4_in[G.p][q], 16 * (G.k + 1))
                        last = dve.tensor_scalar(xn4[G.p][:, q, :], xg[G.p][:, q, 0:F], xg[G.p][:, q, F:F + 1],
                                                 xg[G.p][:, q, F + 1:F + 2], ALU.subtract, ALU.mult)
                    last.then_inc(s4_xn, 1)

                def low_part(G):
                    dve.wait_ge(s4_hi, G.n + 1)
                    dve.tensor_tensor(xT_lo[G.p][:], xT_ps[:], xT_hi[G.p][:], ALU.subtract).then_inc(s4_lo, 1)

                def H_low(k):
                    def body(G):
                        dve.wait_ge(s4_Hhi, KC * G.n + k + 1)
                        dve.tensor_tensor(H_lo[G.p][:, k, :], H_sb[G.p][:, k, :], H_hi[G.p][:, k, :], ALU.subtract
                                          ).then_inc(s4_Hlo, 1)
                    return body

                def combine(tiles):
                    def body(G):
                        if 0 in tiles:
                            if from_group(G, 3):
                                dve.wait_ge(s4_out[G.p], 16 * Q * G.k)
                            dve.tensor_copy(idx_out[G.p][:], xg[G.p][:, :, ROW - 1])
                        for q in tiles:
                            dve.wait_ge(s4_y, Q * G.n + q + 1)
                            dve.scalar_tensor_tensor(
                                yo[G.p][:, q, :], y_ps[(G.p + q) % NB4][:, 0:F],
                                xg[G.p][:, q, F + 2:F + 3], xg[G.p][:, q, 0:F], ALU.mult, ALU.add
                            ).then_inc(s4_yo, 1)
                    return body

                run_stages(dve, SGROUPS, NB4, START4, [
                    (3, H_low(3)), (1, normalise), (2, H_low(1)), (3, combine((0, 1))), (1, low_part),
                    (2, H_low(2)), (3, combine((2, 3)))])


_INS = ["x", "adj", "L0_gnn_W", "L0_gnn_a", "L0_ffn_W1", "L0_ffn_b1", "L0_ffn_Wg", "L0_ffn_bg",
        "L0_ffn_Wd", "L0_ffn_bd"]


def kernel(**inputs):
    import numpy as np
    import concourse.bacc as bacc
    from concourse.bass_utils import run_bass_kernel_spmd

    nc = bacc.Bacc("TRN2", target_bir_lowering=False, num_devices=1)
    arrays, args = {}, []
    for name in _INS:
        v = np.ascontiguousarray(inputs[name])
        if name == "x":
            v = v.reshape(B * N, F)
        arrays[f"in_{name}"] = v
        args.append(nc.dram_tensor(f"in_{name}", v.shape, mybir.dt.from_np(v.dtype), kind="ExternalInput").ap())
    out = nc.dram_tensor("out", (B * N, F), F32, kind="ExternalOutput").ap()
    build(nc, *args, out)
    r = run_bass_kernel_spmd(nc, [arrays], core_ids=[0])
    return r.results[0]["out"].reshape(B, N, F)
```

```python
from collections import namedtuple
from contextlib import ExitStack

import concourse.bass as bass
from concourse import mybir

ALU = mybir.AluOpType
ACT = mybir.ActivationFunctionType
AX = mybir.AxisListType
F32 = mybir.dt.float32
F16 = mybir.dt.float16
BF16 = mybir.dt.bfloat16
I32 = mybir.dt.int32
U32 = mybir.dt.uint32
MAX = bass.bass_isa.ReduceOp.max

P = 128
BANK = 512
B, N, F = 32, 256, 128
H, D = 4, 32
HID, E = 512, 8
KC = HID // P
TILES = B * N // P
Q = 4
GT = Q * P
GROUPS = TILES // Q
GB = GT // N
JT = N // P
D1 = D + 1
EPS = 1e-5
SCALE_LN = 10 * 0.6931471805599453
START1 = 6
SLOTS = TILES + E
SGROUPS = SLOTS // Q
LIST = B * N + P
NOBODY = B * N
ROW = F + 4
STEEP = 2.0 ** 100
LO = 32
W_SCALE = 2.0 ** 8

Group = namedtuple("Group", "n k p")


Phase = namedtuple("Phase", "groups buffers start stages")


def run_stages(eng, *phases):

    def peeled(phase, t):
        for lag, body in phase.stages:
            n = t - lag
            if 0 <= n < phase.groups:
                body(Group(n, n // phase.buffers, n % phase.buffers))

    ending = []
    for phase in phases:
        beginning = list(range(phase.start))
        if ending:
            peeled(*ending.pop(0))
        while ending or beginning:
            if ending:
                peeled(*ending.pop(0))
            if beginning:
                peeled(phase, beginning.pop(0))
        buffers = phase.buffers
        with eng.Fori(phase.start // buffers, phase.groups // buffers) as i:
            for u in range(buffers):
                for lag, body in phase.stages:
                    body(Group(buffers * i + (u - lag), i + (u - lag) // buffers, (u - lag) % buffers))
        last = max(lag for lag, _ in phase.stages)
        ending = [(phase, t) for t in range(phase.groups, phase.groups + last)]
    for step in ending:
        peeled(*step)


def from_group(G, first):
    return not isinstance(G.n, int) or G.n >= first


def wait_apart(eng, sem, value, passed):
    eng.wait_ge(sem, value)
    eng.sem_inc(passed, 1)


def build(nc, x, adj, W, a, W1, b1, Wg, bg, Wd, bd, out):
    ctx = ExitStack()
    with ctx:
        def sb(name, shape, dt=F32):
            return ctx.enter_context(nc.sbuf_tensor(name, shape, dt))

        phases123 = ctx.enter_context(ExitStack())

        def sb1(name, shape, dt=F32):
            return phases123.enter_context(nc.sbuf_tensor(name, shape, dt))

        def sem(name):
            return ctx.enter_context(nc.semaphore(name))

        lists = nc.dram_tensor("lists", (E * LIST + P, ROW), F32, kind="Internal").ap()

        x_all = sb("x_all", [P, TILES, F])
        ident = sb("ident", [P, P])
        Wd_sb = sb("Wd_sb", [P, E * KC, F])
        Wd_hi = sb("Wd_hi", [P, E * KC, F], F16)
        Wd_lo = sb("Wd_lo", [P, E * KC, F], F16)
        bd_sb = sb("bd_sb", [LO + 1, E * KC, F // KC])
        bd2 = sb("bd2", [LO + 1, E * KC, F // KC], F16)
        W1_sb = sb("W1_sb", [P, HID])
        b1_sb = sb("b1_sb", [P, KC])
        Wg_sb = sb("Wg_sb", [P, KC, E])
        bg_sb = sb("bg_sb", [E, 1])
        mhalf = sb("mhalf", [P, Q])
        ones16 = sb("ones16", [P, P], F16)
        expert_i = sb("expert_i", [1, SLOTS], I32)
        start_i = sb("start_i", [1, SLOTS], I32)
        W1_hi = sb("W1_hi", [P, HID], F16)
        W1_lo = sb("W1_lo", [P, HID], F16)
        ones = sb1("ones", [P, Q, F])
        stats = [sb1(f"stats{i}", [P, Q, 6]) for i in range(2)]
        mv = [sb1(f"mv{i}", [P, Q, 2]) for i in range(2)]
        veps = [sb1(f"veps{i}", [P, Q]) for i in range(2)]
        rstd = [sb1(f"rstd{i}", [P, Q]) for i in range(2)]
        xn = [sb1(f"xn{i}", [P, Q, F]) for i in range(2)]
        adj_i = sb1("adj_i", [P, JT, N], I32)
        adj_f = sb1("adj_f", [P, JT, N])
        mask = sb1("mask", [P, JT, N], BF16)
        negmask = sb1("negmask", [P, JT, N], BF16)
        a_sb = sb1("a_sb", [P, H, 2, D])
        wa_prod = sb1("wa_prod", [P, 2, H, D])
        Wcat = sb1("Wcat", [P, F + 3 * H])
        Wa1rep = sb1("Wa1rep", [P, H, P])
        xTs = [sb1(f"xTs{i}", [P, GT]) for i in range(2)]
        eh = [sb1(f"eh{i}", [P, 3, Q, H]) for i in range(2)]
        emax = [sb1(f"emax{i}", [P, GB, H]) for i in range(2)]
        guard = [sb1(f"guard{i}", [P, GB, H]) for i in range(2)]
        shifted = [sb1(f"shifted{i}", [P, 2, Q, H]) for i in range(2)]
        args = [sb1(f"args{i}", [P, 3, Q, H]) for i in range(2)]
        ex = [sb1(f"ex{i}", [P, 3, Q, H]) for i in range(2)]
        V = [sb1(f"V{i}", [P, Q, H, 2, D1]) for i in range(2)]
        Vhi = [sb1(f"Vhi{i}", [P, Q, H, 2, D1], F16) for i in range(2)]
        Vlo = [sb1(f"Vlo{i}", [P, Q, H, 2, D1], F16) for i in range(2)]
        steep = [sb1(f"steep{i}", [P, GB, JT, N], BF16) for i in range(2)]
        C = [sb1(f"C{i}", [P, H, GB, JT, N], BF16) for i in range(2)]
        rB = sb1("rB", [P, Q, H, D1])
        num = [sb1(f"num{i}", [P, Q, H, D1]) for i in range(2)]
        rden = [sb1(f"rden{i}", [P, Q, H]) for i in range(2)]
        hh = [sb1(f"hh{i}", [P, Q, F]) for i in range(2)]
        eh_exp = [sb1(f"eh_exp{i}", [P, Q, F]) for i in range(2)]
        xm1 = [sb1(f"xm1{i}", [P, Q, F]) for i in range(2)]
        x_relu = sb1("x_relu", [P, Q, F])

        psum = ctx.enter_context(nc.psum_tensor("psum", [P, 8, BANK], F32))
        bank = [psum[:, i, :] for i in range(8)]
        xT_ps = bank[0]
        Wh_ps = psum[:, 1:3, :].rearrange("p b (t c) -> p (b t) c", t=2)
        ei_ps = [bank[3], bank[4], bank[3], bank[7]]
        agg_ps = psum[:, 5:7, 0:H * 2 * D1].rearrange("p b (h t d) -> p b h t d", h=H, t=2)
        setup_ps = bank[7]

        s_w = sem("weights_loaded")
        s_passed = sem("waits_passed")
        s_adj = sem("adj_loaded")
        s_x = [sem("x_loaded0"), sem("x_loaded1")]
        s_const = sem("constants_ready")
        s_bd = sem("bd_cleared")
        s_adjf = sem("adj_float")
        s_adjT = sem("adj_transposed")
        s_mask = sem("mask_ready")
        s_wa = sem("wa_ready")
        s_bn = sem("stats_of_tiles")
        s_mv = sem("mean_var_ready")
        s_veps = sem("var_eps")
        s_rstd = sem("rstd_ready")
        s_xn = sem("normalised")
        s_xT = sem("transposed")
        s_xTs = sem("transposed_in_sbuf")
        s_wh = sem("wh_ready")
        s_ei = sem("ei_broadcast")
        s_eh = sem("e_in_sbuf")
        s_emax = sem("e_max_of_tiles")
        s_guard = sem("guard_ready")
        s_shift = sem("e_shifted")
        s_args = sem("exp_args_ready")
        s_ex = sem("exps_ready")
        s_V = sem("V_ready")
        s_Vhi = sem("V_high_part")
        s_Vlo = sem("V_low_part")
        s_steep = sem("steep_of_heads")
        s_C = sem("C_of_heads")
        s_agg = sem("sums_of_tiles")
        s_rB = sem("rB_of_tiles")
        s_num = sem("numerators_of_tiles")
        s_rden = sem("denominator_inverted")
        s_hh = sem("h_ready")
        s_eexp = sem("exp_h_ready")
        s_xm1 = sem("x_minus_1")
        s_relu = sem("x_plus_relu")
        s_x2 = sem("x2_ready")

        H_sb = [sb1(f"H{i}", [P, KC, GT]) for i in range(2)]
        stats2 = [sb1(f"p2_stats{i}", [P, Q, 6]) for i in range(2)]
        mv2 = [sb1(f"p2_mv{i}", [P, Q, 2]) for i in range(2)]
        veps2 = [sb1(f"p2_veps{i}", [P, Q]) for i in range(2)]
        xn2 = [sb1(f"p2_xn{i}", [P, Q, F]) for i in range(2)]
        h_ps = bank[1:5]
        gate_ps = bank[5]
        logit_ps = bank[7]
        rank_ps = bank[6]
        total_ps = bank[7]
        xT_hi = [sb1(f"xT_hi{i}", [P, GT], F16) for i in range(2)]
        xT_lo = [sb1(f"xT_lo{i}", [P, GT], F16) for i in range(2)]
        iota_e = sb1("iota_e", [P, E])
        base_e = sb1("base_e", [P, E])
        before = sb1("before", [P, P], F16)
        meta = sb1("meta", [P, TILES, 4])
        lgT = [sb1(f"lgT{i}", [E, GT]) for i in range(2)]
        top = sb1("top", [P, Q])
        below = [sb1(f"below{i}", [P, Q, E]) for i in range(2)]
        cand = sb1("cand", [P, Q, E])
        first = sb1("first", [P, Q])
        hot = [sb1(f"hot{i}", [P, Q, E], F16) for i in range(2)]
        hot_all = sb1("hot_all", [P, E], F16)
        hot_sum = [sb1(f"hot_sum{i}", [P, E], F16) for i in range(2)]
        half_tanh = [sb1(f"half_tanh{i}", [P, Q, E]) for i in range(2)]
        less = sb1("less", [P, Q, E])
        part = sb1("part", [P, Q, E])
        total = sb1("total", [P, Q])
        total_exp = sb1("total_exp", [P, Q])
        ranked = sb1("ranked", [P, Q, E])
        masked = sb1("masked", [P, Q, E])
        place = [sb1(f"place{i}", [P, Q], U32) for i in range(2)]
        place_f = sb1("place_f", [P, Q])
        rows = [sb1(f"rows{i}", [P, Q, ROW]) for i in range(2)]
        nobody = sb1("nobody", [P, ROW])

        s2_const = sem("p2_constants")
        s2_bn = sem("p2_stats_of_tiles")
        s2_mv = sem("p2_mean_var_ready")
        s2_veps = sem("p2_var_eps")
        s2_rstd = sem("p2_rstd_ready")
        s2_meta = sem("p2_meta_kept")
        s2_xn = sem("p2_normalised")
        s2_xT = sem("p2_transposed")
        s2_hi = sem("p2_high_part")
        s2_lo = sem("p2_low_part")
        s2_h = sem("p2_hidden_chunks")
        s2_gelu = sem("p2_gelu_chunks")
        s2_gate = sem("p2_gate_logits")
        s2_lgT = sem("p2_logits_in_sbuf")
        s2_logit = sem("p2_logits_of_tokens")
        s2_top = sem("p2_top_chain")
        s2_below = sem("p2_logits_below_top")
        s2_hot = sem("p2_onehot_ready")
        s2_sum = sem("p2_onehot_sums")
        s2_tanh = sem("p2_tanh_ready")
        s2_gate_step = sem("p2_gate_chain")
        s2_rank = sem("p2_ranks_ready")
        s2_ranked = sem("p2_ranks_chain")
        s2_place = sem("p2_places_ready")
        s2_x = sem("p2_x_in_rows")
        s2_rows = sem("p2_rows_ready")
        s2_put = [sem("p2_rows_stored0"), sem("p2_rows_stored1")]
        s2_nobody = sem("p2_nobody_stored")
        s2_hot_all = sem("p2_onehots_of_group_summed")
        s2_total = sem("p2_totals")
        s2_wd = sem("p2_expert_weights_split")
        START2 = 8

        slot_f = sb1("slot_f", [1, SLOTS])
        count = sb1("count", [1, E])
        count_i = sb1("count_i", [1, E], I32)
        blocks_i = sb1("blocks_i", [1, E], I32)
        blocks_f = sb1("blocks_f", [1, E])
        cum = [sb1(f"cum{i}", [1, E]) for i in range(2)]
        room = sb1("room", [1, E])
        tail_f = sb1("tail_f", [1, E])
        tail_i = sb1("tail_i", [1, E], I32)
        past = sb1("past", [1, SLOTS, E])
        jumps = sb1("jumps", [1, SLOTS, E])
        expert_f = sb1("expert_f", [1, SLOTS])
        start_f = sb1("start_f", [1, SLOTS])

        s3_const = sem("p3_constants")
        s3 = sem("p3_vector_step")
        s3_tail = sem("p3_tails_ready")
        s3_fill = sem("p3_tails_stored")

        def fill(eng, experts):
            eng.wait_ge(s2_const, 8)
            eng.wait_ge(s3_tail, 1)
            for e in experts:
                tail = eng.value_load(tail_i[0:1, e:e + 1], min_val=0, max_val=E * LIST - P)
                eng.dma_start(lists[bass.ds(tail, P), :], nobody[:]).then_inc(s3_fill, 16)
            eng.wait_ge(s3_fill, 16 * E)

        WLOADS = 10
        with nc.Block() as block:
            @block.sync
            def _(sp):
                sp.dma_start(adj_i[:], adj.rearrange("(t p) j -> p t j", p=P)).then_inc(s_adj, 16)
                with nc.allow_non_contiguous_dma(reason="small weights, once"):
                    sp.dma_start(Wcat[:, 0:F].rearrange("p (h d) -> p h d", h=H),
                                 W.rearrange("h f d -> f h d")).then_inc(s_w, 16)
                    sp.dma_start(a_sb[:].rearrange("p h t d -> p (h t d)"),
                                 a.rearrange("h t -> (h t)").partition_broadcast(P)).then_inc(s_w, 16)
                    sp.dma_start(b1_sb[:], b1.rearrange("(k p) -> p k", p=P)).then_inc(s_w, 16)
                    sp.dma_start(Wg_sb[:], Wg.rearrange("(k p) e -> p k e", p=P)).then_inc(s_w, 16)
                    sp.dma_start(bg_sb[:], bg.rearrange("(e o) -> e o", o=1)).then_inc(s_w, 16)

                def load_x(G):
                    if from_group(G, 2):
                        sp.wait_ge(s_mv, G.n - 1)
                    sp.dma_start(x_all[:, bass.ds(G.n * Q, Q), 0:F],
                                 x[bass.ds(G.n * GT, GT), :].rearrange("(t p) f -> p t f", p=P)
                                 ).then_inc(s_x[G.p], 16)

                run_stages(sp, Phase(GROUPS, 2, 4, [(0, load_x)]))
                sp.wait_ge(s2_const, 8)
                sp.dma_start(lists[E * LIST:E * LIST + P, :], nobody[:]).then_inc(s2_nobody, 16)
                sp.wait_ge(s2_nobody, 16)

                fill(sp, range(0, E, 2))

            @block.gpsimd
            def _(pool):
                pool.memset(bd_sb[:], 0.0).then_inc(s_bd, 1)
                pool.memset(ident[:], 1.0).then_inc(s_const, 1)
                pool.memset(mhalf[:], -0.5).then_inc(s_const, 1)
                pool.memset(ones[:], 1.0).then_inc(s_const, 1)
                pool.wait_ge(s_const, 1)
                pool.affine_select(out=ident[:], in_=ident[:], compare_op=ALU.is_equal, fill=0.0,
                                   base=0, pattern=[[-1, P]], channel_multiplier=1).then_inc(s_const, 1)

                def rstd_of(G):
                    wait_apart(pool, s_mv, G.n + 1, s_passed)
                    pool.tensor_scalar(veps[G.p][:], mv[G.p][:, :, 1], EPS, None, ALU.add).then_inc(s_veps, 1)
                    pool.wait_ge(s_veps, G.n + 1)
                    pool.tensor_tensor(rstd[G.p][:], veps[G.p][:], mhalf[:], ALU.pow).then_inc(s_rstd, 1)

                def guard_args(G):
                    wait_apart(pool, s_emax, G.n + 1, s_passed)
                    pool.partition_all_reduce(guard[G.p][:].rearrange("p b h -> p (b h)"),
                                              emax[G.p][:].rearrange("p b h -> p (b h)"), P, MAX
                                              ).then_inc(s_guard, 1)
                    pool.wait_ge(s_guard, G.n + 1)
                    for b in range(GB):
                        g_b = guard[G.p][:, b:b + 1, :].broadcast_to([P, JT, H])
                        t_b = slice(b * JT, (b + 1) * JT)
                        pool.tensor_tensor(shifted[G.p][:, 0, t_b, :], eh[G.p][:, 0, t_b, :], g_b, ALU.subtract)
                        last = pool.tensor_tensor(shifted[G.p][:, 1, t_b, :], eh[G.p][:, 1, t_b, :], g_b, ALU.add)
                    last.then_inc(s_shift, 1)
                    wait_apart(pool, s_shift, G.n + 1, s_passed)
                    pool.tensor_scalar(args[G.p][:, 0], shifted[G.p][:, 0], 1.0, SCALE_LN, ALU.mult, ALU.add)
                    pool.tensor_scalar(args[G.p][:, 1], shifted[G.p][:, 0], 0.2, SCALE_LN, ALU.mult, ALU.add)
                    pool.tensor_scalar(args[G.p][:, 2], shifted[G.p][:, 1], 0.0, -0.8, ALU.max, ALU.mult
                                       ).then_inc(s_args, 1)

                def V_low(G):
                    pool.wait_ge(s_V, G.n + 1)
                    pool.wait_ge(s_Vhi, G.n + 1)
                    flat = "p q h t d -> p (q h t d)"
                    pool.tensor_tensor(Vlo[G.p][:].rearrange(flat), V[G.p][:].rearrange(flat),
                                       Vhi[G.p][:].rearrange(flat), ALU.subtract).then_inc(s_Vlo, 1)

                def x_minus_1(G):
                    if from_group(G, 2):
                        pool.wait_ge(s_x2, G.n - 1)
                    pool.tensor_tensor(xm1[G.p][:], x_all[:, bass.ds(G.n * Q, Q), 0:F], ones[:], ALU.subtract
                                       ).then_inc(s_xm1, 1)

                def h_out(G):
                    pool.wait_ge(s_rden, G.n + 1)
                    pool.tensor_tensor(hh[G.p][:].rearrange("p q (h d) -> p (q h) d", h=H),
                                       num[G.p][:, :, :, 0:D].rearrange("p q h d -> p (q h) d"),
                                       rden[G.p][:].rearrange("p q h -> p (q h)").unsqueeze(2).broadcast_to([P, Q * H, D]),
                                       ALU.mult).then_inc(s_hh, 1)


                pool.memset(nobody[:], 0.0).then_inc(s2_const, 1)
                pool.memset(ones16[:], 1.0).then_inc(s2_const, 1)
                pool.memset(hot_sum[0][:], 0.0).then_inc(s2_const, 1)
                pool.iota(iota_e[:], pattern=[[1, E]], base=-E, channel_multiplier=0,
                          allow_small_or_imprecise_dtypes=True).then_inc(s2_const, 1)
                pool.iota(base_e[:], pattern=[[LIST, E]], base=0, channel_multiplier=0,
                          allow_small_or_imprecise_dtypes=True).then_inc(s2_const, 1)
                pool.iota(meta[:, :, 3], pattern=[[P, TILES]], base=0, channel_multiplier=1,
                          allow_small_or_imprecise_dtypes=True).then_inc(s2_const, 1)
                pool.wait_ge(s2_const, 6)
                pool.memset(nobody[:, ROW - 1:ROW], float(NOBODY)).then_inc(s2_const, 1)
                pool.affine_select(out=before[:], in_=ones16[:], compare_op=ALU.is_gt, fill=0.0, base=0,
                                   pattern=[[1, P]], channel_multiplier=-1).then_inc(s2_const, 1)

                pool.iota(slot_f[:], pattern=[[P, SLOTS]], base=0, channel_multiplier=0,
                          allow_small_or_imprecise_dtypes=True).then_inc(s3_const, 1)

                def rstd_of2(G):
                    wait_apart(pool, s2_mv, G.n + 1, s_passed)
                    pool.tensor_scalar(veps2[G.p][:], mv2[G.p][:, :, 1], EPS, None, ALU.add).then_inc(s2_veps, 1)
                    pool.wait_ge(s2_veps, G.n + 1)
                    pool.tensor_tensor(mv2[G.p][:, :, 1], veps2[G.p][:], mhalf[:], ALU.pow).then_inc(s2_rstd, 1)
                    pool.wait_ge(s2_rstd, G.n + 1)
                    pool.tensor_copy(meta[:, bass.ds(G.n * Q, Q), 0:2], mv2[G.p][:]).then_inc(s2_meta, 1)

                def put(G):
                    pool.wait_ge(s2_place, G.n + 1)
                    pool.tensor_copy(rows[G.p][:, :, F:ROW], meta[:, bass.ds(G.n * Q, Q), :]).then_inc(s2_rows, 1)
                    wait_apart(pool, s2_x, G.n + 1, s_passed)
                    wait_apart(pool, s2_rows, G.n + 1, s_passed)
                    for q in range(Q):
                        pool.indirect_dma_start(
                            out=lists[:, :], out_offset=bass.IndirectOffsetOnAxis(ap=place[G.p][:, q:q + 1], axis=0),
                            in_=rows[G.p][:, q, :], in_offset=None).then_inc(s2_put[G.p], 16)

                run_stages(pool,
                           Phase(GROUPS, 2, START1, [
                    (2, V_low), (0, rstd_of), (1, guard_args), (3, h_out), (3, x_minus_1)]),
                           Phase(GROUPS, 2, START2, [(5, put), (0, rstd_of2)]))
                for i in range(2):
                    pool.wait_ge(s2_put[i], 16 * Q * GROUPS // 2)

            @block.scalar
            def _(act):
                act.dma_start(W1_sb[:], W1[:, :]).then_inc(s_w, 16)
                for half in range(2):
                    act.dma_start(Wd_sb[:, half * 16:(half + 1) * 16, :],
                                  Wd[half * 4:(half + 1) * 4].rearrange("e (k p) c -> p (e k) c", p=P)
                                  ).then_inc(s_w, 16)
                act.wait_ge(s_bd, 1)
                for part in (0, LO):
                    act.dma_start(bd_sb[part:part + 1].rearrange("p k c -> p (k c)"),
                                  bd.rearrange("(o e) c -> o (e c)", o=1)).then_inc(s_w, 16)

                def xT_out(G):
                    act.wait_ge(s_xT, G.n + 1)
                    if from_group(G, 2):
                        act.wait_ge(s_ei, H * (G.n - 1))
                    act.activation(xTs[G.p][:], xT_ps[:], ACT.Copy).then_inc(s_xTs, 1)

                def exps(G):
                    act.wait_ge(s_args, G.n + 1)
                    if from_group(G, 2):
                        act.wait_ge(s_num, Q // 2 * (G.n - 1))
                    act.activation(ex[G.p][:].rearrange("p t q h -> p (t q h)"),
                                   args[G.p][:].rearrange("p t q h -> p (t q h)"), ACT.Exp).then_inc(s_ex, 1)

                def V_high(G):
                    act.wait_ge(s_V, G.n + 1)
                    if from_group(G, 2):
                        act.wait_ge(s_agg, Q * (G.n - 1))
                    flat = "p q h t d -> p (q h t d)"
                    act.activation(Vhi[G.p][:].rearrange(flat), V[G.p][:].rearrange(flat), ACT.Copy).then_inc(s_Vhi, 1)

                def exp_h(G):
                    act.wait_ge(s_hh, G.n + 1)
                    act.activation(eh_exp[G.p][:], hh[G.p][:], ACT.Exp).then_inc(s_eexp, 1)

                def steep_heads(heads):
                    def body(G):
                        for h in heads:
                            act.wait_ge(s_ei, H * G.n + h + 1)
                            if h == 0:
                                act.wait_ge(s_eh, G.n + 1)
                            if from_group(G, 1) or h >= 2:
                                act.wait_ge(s_C, H * G.n + h - 1)
                            for b in range(GB):
                                for jt in range(JT):
                                    last = act.activation(steep[h % 2][:, b, jt, :], ei_ps[h][:, b * N:(b + 1) * N],
                                                          ACT.Relu, bias=eh[G.p][:, 2, JT * b + jt, h:h + 1], scale=STEEP)
                            last.then_inc(s_steep, 1)
                    return body


                def high_part(G):
                    act.wait_ge(s2_xT, G.n + 1)
                    if from_group(G, 2):
                        act.wait_ge(s2_h, KC * (G.n - 1))
                    act.activation(xT_hi[G.p][:], xT_ps[:], ACT.Copy).then_inc(s2_hi, 1)

                def gelu(G):
                    if from_group(G, 2):
                        act.wait_ge(s2_gate, G.n - 1)
                    for k in range(KC):
                        act.wait_ge(s2_h, KC * G.n + k + 1)
                        act.activation(H_sb[G.p][:, k, :], h_ps[k][:], ACT.Gelu, bias=b1_sb[:, k:k + 1],
                                       scale=1.0 / W_SCALE).then_inc(s2_gelu, 1)

                def logits_out(G):
                    act.wait_ge(s2_gate, G.n + 1)
                    if from_group(G, 2):
                        act.wait_ge(s2_logit, G.n - 1)
                    act.activation(lgT[G.p][:], gate_ps[0:E, :], ACT.Identity, bias=bg_sb[:]).then_inc(s2_lgT, 1)

                def tanh(G):
                    act.wait_ge(s2_below, G.n + 1)
                    if from_group(G, 2):
                        act.wait_ge(s2_gate_step, 4 * (G.n - 1))
                    act.activation(half_tanh[G.p][:], below[G.p][:], ACT.Tanh, scale=0.5).then_inc(s2_tanh, 1)

                def x_in_rows(G):
                    if not from_group(G, 1):
                        act.wait_ge(s_x2, GROUPS)
                    if from_group(G, 2):
                        act.wait_ge(s2_put[G.p], 16 * Q * G.k)
                    act.activation(rows[G.p][:, :, 0:F], x_all[:, bass.ds(G.n * Q, Q), :], ACT.Copy).then_inc(s2_x, 1)

                act.wait_ge(s_w, 16 * WLOADS)
                for part8 in range(4):
                    c = slice(part8 * KC * 2, (part8 + 1) * KC * 2)
                    act.activation(Wd_hi[:, c, :], Wd_sb[:, c, :], ACT.Copy, scale=W_SCALE)
                act.activation(bd2[:], bd_sb[:], ACT.Copy, scale=W_SCALE).then_inc(s2_wd, 1)
                run_stages(act,
                           Phase(GROUPS, 2, START1, [
                    (2, steep_heads((0,))), (1, xT_out), (2, V_high), (2, steep_heads((1,))), (4, exp_h),
                    (2, steep_heads((2, 3))), (1, exps)]),
                           Phase(GROUPS, 2, START2, [
                               (4, logits_out), (5, x_in_rows), (2, gelu), (1, high_part), (4, tanh)]))

                fill(act, range(1, E, 2))

            @block.tensor
            def _(pe):
                pe.wait_ge(s_const, 4)
                pe.wait_ge(s_adjf, 1)
                for jt in range(JT):
                    for it in range(JT):
                        last = pe.transpose(setup_ps[:, jt * N + it * P:jt * N + (it + 1) * P],
                                            adj_f[:, it, jt * P:(jt + 1) * P], ident[:])
                last.then_inc(s_adjT, 1)

                def transposes(G):
                    pe.wait_ge(s_xn, G.n + 1)
                    if from_group(G, 1):
                        pe.wait_ge(s_xTs, G.n)
                    for q in range(Q):
                        last = pe.transpose(xT_ps[:, q * P:(q + 1) * P], xn[G.p][:, q, :], ident[:])
                    last.then_inc(s_xT, 1)

                def project(G):
                    pe.wait_ge(s_xTs, G.n + 1)
                    if not from_group(G, 1):
                        pe.wait_ge(s_wa, 4)
                    else:
                        pe.wait_ge(s_V, G.n)
                    for q in range(Q):
                        last = pe.matmul(Wh_ps[:, q, 0:F + 3 * H], xTs[G.p][:, q * P:(q + 1) * P],
                                         Wcat[:], start=True, stop=True)
                    last.then_inc(s_wh, 1)

                def ei_heads(heads):
                    def body(G):
                        for h in heads:
                            if h in (0, 2) and (from_group(G, 1) or h == 2):
                                pe.wait_ge(s_steep, H * G.n + h - 1)
                            if h in (1, 3) and from_group(G, 1):
                                pe.wait_ge(s_steep, H * (G.n - 1) + h + 1)
                            pe.matmul(ei_ps[h][:], Wa1rep[:, h, :], xTs[G.p][:], start=True, stop=True
                                      ).then_inc(s_ei, 1)
                    return body

                def sum_tiles(tiles):
                    def body(G):
                        if 0 in tiles:
                            pe.wait_ge(s_C, H * (G.n + 1))
                            pe.wait_ge(s_Vlo, G.n + 1)
                        for q in tiles:
                            if q % 2 == 0 and (from_group(G, 1) or q >= 2):
                                pe.wait_ge(s_num, Q // 2 * G.n + q // 2)
                            b, i_cols = q // JT, slice((q % JT) * P, (q % JT + 1) * P)
                            dst = agg_ps[:, q % 2]
                            parts = [(jt, v[G.p]) for jt in range(JT) for v in (Vhi, Vlo)]
                            for n, (jt, v) in enumerate(parts):
                                pe.matmul(dst[:, :, 1, :], negmask[:, jt, i_cols], v[:, JT * b + jt, :, 1, :],
                                          start=(n == 0), stop=False, skip_group_check=True)
                            for h in range(H):
                                for n, (jt, v) in enumerate(parts):
                                    last = pe.matmul(dst[:, h, :, :].rearrange("p t d -> p (t d)"),
                                                     C[G.p][:, h, b, jt, i_cols],
                                                     v[:, JT * b + jt, h, :, :].rearrange("p t d -> p (t d)"),
                                                     start=False, stop=(h == H - 1 and n == 3),
                                                     skip_group_check=True)
                            last.then_inc(s_agg, 1)
                    return body


                def transposes2(G):
                    if not from_group(G, 1):
                        pe.wait_ge(s_xTs, GROUPS)
                    pe.wait_ge(s2_xn, G.n + 1)
                    if from_group(G, 1):
                        pe.wait_ge(s2_lo, G.n)
                    for q in range(Q):
                        last = pe.transpose(xT_ps[:, q * P:(q + 1) * P], xn2[G.p][:, q, :], ident[:])
                    last.then_inc(s2_xT, 1)

                def hidden_chunks(chunks):
                    def body(G):
                        if not from_group(G, 1):
                            pe.wait_ge(s_V, GROUPS)
                            pe.wait_ge(s_steep, H * GROUPS)
                        pe.wait_ge(s2_lo, G.n + 1)
                        for k in chunks:
                            cols = slice(k * P, (k + 1) * P)
                            if from_group(G, 1):
                                pe.wait_ge(s2_gelu, KC * (G.n - 1) + k + 1)
                            pe.matmul(h_ps[k][:], W1_hi[:, cols], xT_lo[G.p][:], start=True, stop=False)
                            pe.matmul(h_ps[k][:], W1_lo[:, cols], xT_hi[G.p][:], start=False, stop=False)
                            pe.matmul(h_ps[k][:], W1_hi[:, cols], xT_hi[G.p][:], start=False, stop=True
                                      ).then_inc(s2_h, 1)
                    return body

                def gate(G):
                    if not from_group(G, 1):
                        pe.wait_ge(s_num, Q // 2 * GROUPS)
                    pe.wait_ge(s2_gelu, KC * (G.n + 1))
                    if from_group(G, 1):
                        pe.wait_ge(s2_lgT, G.n)
                    for k in range(KC):
                        last = pe.matmul(gate_ps[0:E, :], Wg_sb[:, k, :], H_sb[G.p][:, k, :],
                                         start=(k == 0), stop=(k == KC - 1))
                    last.then_inc(s2_gate, 1)

                def logits_back(G):
                    if from_group(G, 1):
                        pe.wait_ge(s2_below, G.n)
                    wait_apart(pe, s2_lgT, G.n + 1, s_passed)
                    for q in range(Q):
                        last = pe.transpose(logit_ps[:, q * E:(q + 1) * E], lgT[G.p][:, q * P:(q + 1) * P],
                                            ident[0:E, 0:E])
                    last.then_inc(s2_logit, 1)

                def rank(G):
                    pe.wait_ge(s2_hot, G.n + 1)
                    if from_group(G, 1):
                        pe.wait_ge(s2_ranked, 3 * (G.n - 1) + 1)
                    flat = "p q e -> p (q e)"
                    pe.matmul(rank_ps[:, 0:Q * E], before[:], hot[G.p][:].rearrange(flat), start=True, stop=False,
                              skip_group_check=True)
                    for q in range(Q - 1):
                        pe.matmul(rank_ps[:, (q + 1) * E:Q * E], ones16[:],
                                  hot[G.p][:, q:q + 1, :].broadcast_to([P, Q - 1 - q, E]), start=False, stop=False,
                                  skip_group_check=True)
                    if from_group(G, 1):
                        pe.wait_ge(s2_sum, G.n)
                    pe.matmul(rank_ps[:, 0:Q * E], ones16[:], hot_sum[G.p][:].unsqueeze(1).broadcast_to([P, Q, E]),
                              start=False, stop=True, skip_group_check=True).then_inc(s2_rank, 1)

                pe.wait_ge(s2_const, 8)
                run_stages(pe,
                           Phase(GROUPS, 2, START1, [
                    (1, transposes), (3, sum_tiles((0, 1))), (2, ei_heads((2,))), (1, project), (2, ei_heads((3,))),
                    (3, sum_tiles((2, 3))), (1, ei_heads((0, 1)))]),
                           Phase(GROUPS, 2, START2, [
                               (2, hidden_chunks((0, 1))), (4, logits_back), (2, hidden_chunks((2, 3))),
                               (1, transposes2), (3, gate), (4, rank)]))
                pe.wait_ge(s2_sum, GROUPS)
                pe.matmul(total_ps[:, 0:E], ones16[:], hot_sum[GROUPS % 2][:], start=True, stop=True
                          ).then_inc(s2_total, 1)

            @block.vector
            def _(dve):
                dve.wait_ge(s_adj, 16)
                dve.tensor_scalar(adj_f[:], adj_i[:], 0.0, None, ALU.is_gt).then_inc(s_adjf, 1)
                dve.wait_ge(s_w, 16 * WLOADS)
                Wv = Wcat[:, 0:F].rearrange("p (h d) -> p h d", h=H)
                for half in range(2):
                    last = dve.tensor_tensor(wa_prod[:, half], Wv, a_sb[:, :, 1 - half, :], ALU.mult)
                last.then_inc(s_wa, 1)
                dve.wait_ge(s_wa, 1)
                dve.tensor_reduce(Wcat[:, F:F + 2 * H].rearrange("p (t h) -> p t h", t=2), wa_prod[:],
                                  AX.X, ALU.add).then_inc(s_wa, 1)
                dve.wait_ge(s_wa, 2)
                dve.tensor_scalar(Wcat[:, F + 2 * H:], Wcat[:, F:F + H], STEEP, None, ALU.mult).then_inc(s_wa, 1)
                dve.tensor_copy(Wa1rep[:], Wcat[:, F + H:F + 2 * H].unsqueeze(2).broadcast_to([P, H, P])
                                ).then_inc(s_wa, 1)
                dve.wait_ge(s_adjT, 1)
                flat = "p t i -> p (t i)"
                dve.tensor_copy(mask[:].rearrange(flat), setup_ps[:])
                dve.tensor_scalar(negmask[:].rearrange(flat), setup_ps[:], -1.0, None, ALU.mult).then_inc(s_mask, 1)
                dve.wait_ge(s_mask, 1)
                dve.tensor_scalar(W1_hi[:], W1_sb[:], W_SCALE, None, ALU.mult).then_inc(s_mask, 1)
                dve.wait_ge(s_mask, 2)
                dve.scalar_tensor_tensor(W1_lo[:], W1_sb[:], W_SCALE, W1_hi[:], ALU.mult, ALU.subtract
                                         ).then_inc(s_mask, 1)

                def stats_of(G):
                    dve.wait_ge(s_x[G.p], 16 * (G.k + 1))
                    for q in range(Q):
                        last = dve.bn_stats(stats[G.p][:, q, :], x_all[:, bass.ds(G.n * Q + q, 1), 0:F].rearrange("p q f -> p (q f)"))
                    last.then_inc(s_bn, 1)
                    wait_apart(dve, s_bn, G.n + 1, s_passed)
                    for q in range(Q):
                        last = dve.bn_aggr(mv[G.p][:, q, :], stats[G.p][:, q, :])
                    last.then_inc(s_mv, 1)

                def normalise(G):
                    dve.wait_ge(s_rstd, G.n + 1)
                    if from_group(G, 2):
                        dve.wait_ge(s_xT, G.n - 1)
                    for q in range(Q):
                        last = dve.tensor_scalar(xn[G.p][:, q, :], x_all[:, bass.ds(G.n * Q + q, 1), 0:F].rearrange("p q f -> p (q f)"),
                                                 mv[G.p][:, q, 0:1], rstd[G.p][:, q:q + 1], ALU.subtract, ALU.mult)
                    last.then_inc(s_xn, 1)

                def e_out(G):
                    dve.wait_ge(s_wh, G.n + 1)
                    dve.tensor_copy(eh[G.p][:], Wh_ps[:, :, F:F + 3 * H].rearrange("p q (t h) -> p t q h", t=3)
                                    ).then_inc(s_eh, 1)
                    dve.wait_ge(s_eh, G.n + 1)
                    ev = eh[G.p][:, 0].rearrange("p (b t) h -> p t b h", b=GB)
                    dve.tensor_tensor(emax[G.p][:], ev[:, 0], ev[:, 1], ALU.max).then_inc(s_emax, 1)

                def C_heads(heads):
                    def body(G):
                        if 0 in heads and from_group(G, 2):
                            dve.wait_ge(s_agg, Q * (G.n - 1))
                        for h in heads:
                            dve.wait_ge(s_steep, H * G.n + h + 1)
                            dve.tensor_tensor(C[G.p][:, h].rearrange("p b t i -> p b (t i)"),
                                              steep[h % 2][:].rearrange("p b t i -> p b (t i)"),
                                              mask[:].rearrange("p t i -> p (t i)").unsqueeze(1).broadcast_to([P, GB, JT * N]),
                                              ALU.min).then_inc(s_C, 1)
                    return body

                def V_out(G):
                    dve.wait_ge(s_ex, G.n + 1)
                    Wh = Wh_ps[:, :, 0:F].rearrange("p q (h d) -> p q h d", h=H)
                    for t in range(2):
                        dve.tensor_tensor(V[G.p][:, :, :, t, 0:D], Wh,
                                          ex[G.p][:, t].unsqueeze(3).broadcast_to([P, Q, H, D]), ALU.mult)
                    dve.tensor_copy(V[G.p][:, :, :, :, D], ex[G.p][:, 0:2].rearrange("p t q h -> p q h t")
                                    ).then_inc(s_V, 1)

                def divide(half):
                    def body(G):
                        two = slice(2 * half, 2 * half + 2)
                        dve.wait_ge(s_agg, Q * G.n + 2 * half + 2)
                        if half == 0 and from_group(G, 2):
                            dve.wait_ge(s_hh, G.n - 1)
                        dve.tensor_tensor(rB[:, two], agg_ps[:, :, :, 1, :],
                                          ex[G.p][:, 2, two, :].unsqueeze(3).broadcast_to([P, 2, H, D1]), ALU.mult
                                          ).then_inc(s_rB, 1)
                        dve.wait_ge(s_rB, Q // 2 * G.n + half + 1)
                        dve.tensor_tensor(num[G.p][:, two], agg_ps[:, :, :, 0, :], rB[:, two], ALU.subtract
                                          ).then_inc(s_num, 1)
                    return body

                def invert(G):
                    dve.wait_ge(s_num, Q // 2 * (G.n + 1))
                    dve.reciprocal(rden[G.p][:], num[G.p][:, :, :, D]).then_inc(s_rden, 1)

                def add_elu(G):
                    if from_group(G, 1):
                        dve.wait_ge(s_x2, G.n)
                    dve.wait_ge(s_xm1, G.n + 1)
                    dve.wait_ge(s_hh, G.n + 1)
                    dve.scalar_tensor_tensor(x_relu[:], hh[G.p][:], 0.0, xm1[G.p][:], ALU.max, ALU.add
                                             ).then_inc(s_relu, 1)
                    dve.wait_ge(s_relu, G.n + 1)
                    dve.wait_ge(s_eexp, G.n + 1)
                    dve.scalar_tensor_tensor(x_all[:, bass.ds(G.n * Q, Q), 0:F], eh_exp[G.p][:], 1.0, x_relu[:],
                                             ALU.min, ALU.add).then_inc(s_x2, 1)


                def stats_of2(G):
                    if not from_group(G, 6):
                        dve.wait_ge(s_x2, G.n + 1 if G.n < 5 else GROUPS)
                    if from_group(G, 2):
                        dve.wait_ge(s2_meta, G.n - 1)
                    for q in range(Q):
                        last = dve.bn_stats(stats2[G.p][:, q, :],
                                            x_all[:, bass.ds(G.n * Q + q, 1), :].rearrange("p q f -> p (q f)"))
                    last.then_inc(s2_bn, 1)
                    wait_apart(dve, s2_bn, G.n + 1, s_passed)
                    for q in range(Q):
                        last = dve.bn_aggr(mv2[G.p][:, q, :], stats2[G.p][:, q, :])
                    last.then_inc(s2_mv, 1)

                def normalise2(G):
                    dve.wait_ge(s2_rstd, G.n + 1)
                    if from_group(G, 2):
                        dve.wait_ge(s2_xT, G.n - 1)
                    for q in range(Q):
                        last = dve.tensor_scalar(xn2[G.p][:, q, :],
                                                 x_all[:, bass.ds(G.n * Q + q, 1), :].rearrange("p q f -> p (q f)"),
                                                 mv2[G.p][:, q, 0:1], mv2[G.p][:, q, 1:2], ALU.subtract, ALU.mult)
                    last.then_inc(s2_xn, 1)

                def low_part(G):
                    dve.wait_ge(s2_hi, G.n + 1)
                    dve.tensor_tensor(xT_lo[G.p][:], xT_ps[:], xT_hi[G.p][:], ALU.subtract).then_inc(s2_lo, 1)

                def over_e(ap):
                    return ap.unsqueeze(2).broadcast_to([P, Q, E])

                def over_q(ap):
                    return ap.unsqueeze(1).broadcast_to([P, Q, E])

                def choose(G):
                    logits = logit_ps[:, 0:Q * E].rearrange("p (q e) -> p q e", q=Q)
                    dve.wait_ge(s2_logit, G.n + 1)
                    dve.tensor_reduce(top[:], logits, AX.X, ALU.max).then_inc(s2_top, 1)
                    dve.wait_ge(s2_top, 3 * G.n + 1)
                    if from_group(G, 2):
                        dve.wait_ge(s2_tanh, G.n - 1)
                    dve.tensor_tensor(below[G.p][:], logits, over_e(top[:]), ALU.subtract).then_inc(s2_below, 1)
                    dve.wait_ge(s2_below, G.n + 1)
                    dve.scalar_tensor_tensor(cand[:], below[G.p][:], 0.0, over_q(iota_e[:]), ALU.is_equal, ALU.mult
                                             ).then_inc(s2_top, 1)

                def one_hot(G):
                    dve.wait_ge(s2_top, 3 * G.n + 2)
                    dve.tensor_reduce(first[:], cand[:], AX.X, ALU.min).then_inc(s2_top, 1)
                    dve.wait_ge(s2_top, 3 * G.n + 3)
                    if from_group(G, 2):
                        dve.wait_ge(s2_rank, G.n - 1)
                    dve.tensor_tensor(hot[G.p][:], over_q(iota_e[:]), over_e(first[:]), ALU.is_equal).then_inc(s2_hot, 1)

                def sum_up(G):
                    dve.wait_ge(s2_hot, G.n + 1)
                    if from_group(G, 1):
                        dve.wait_ge(s2_sum, G.n)
                    with nc.allow_low_precision("counts up to the number of tiles"):
                        dve.tensor_reduce(hot_all[:], hot[G.p][:].rearrange("p q e -> p e q"), AX.X, ALU.add
                                          ).then_inc(s2_hot_all, 1)
                    dve.wait_ge(s2_hot_all, G.n + 1)
                    if from_group(G, 1):
                        dve.wait_ge(s2_rank, G.n)
                    dve.tensor_tensor(hot_sum[1 - G.p][:], hot_sum[G.p][:], hot_all[:], ALU.add).then_inc(s2_sum, 1)

                def places(G):
                    chain, gates = 3 * G.n, 4 * G.n
                    dve.wait_ge(s2_rank, G.n + 1)
                    dve.tensor_tensor(ranked[:], rank_ps[:, 0:Q * E].rearrange("p (q e) -> p q e", q=Q),
                                      over_q(base_e[:]), ALU.add).then_inc(s2_ranked, 1)
                    dve.wait_ge(s2_tanh, G.n + 1)
                    dve.tensor_scalar(less[:], half_tanh[G.p][:], -1.0, 1.0, ALU.mult, ALU.add).then_inc(s2_gate_step, 1)
                    dve.wait_ge(s2_ranked, chain + 1)
                    dve.tensor_tensor(masked[:], ranked[:], hot[G.p][:], ALU.mult).then_inc(s2_ranked, 1)
                    dve.wait_ge(s2_gate_step, gates + 1)
                    dve.reciprocal(part[:], less[:]).then_inc(s2_gate_step, 1)
                    dve.wait_ge(s2_ranked, chain + 2)
                    dve.tensor_reduce(place_f[:], masked[:], AX.X, ALU.add).then_inc(s2_ranked, 1)
                    dve.wait_ge(s2_gate_step, gates + 2)
                    dve.tensor_reduce(total[:], part[:], AX.X, ALU.add).then_inc(s2_gate_step, 1)
                    dve.wait_ge(s2_ranked, chain + 3)
                    if from_group(G, 2):
                        dve.wait_ge(s2_put[G.p], 16 * Q * G.k)
                    dve.tensor_copy(place[G.p][:], place_f[:])
                    dve.wait_ge(s2_gate_step, gates + 3)
                    dve.tensor_scalar(total_exp[:], total[:], 2.0 * W_SCALE, -E * W_SCALE, ALU.mult, ALU.add).then_inc(s2_gate_step, 1)
                    dve.wait_ge(s2_gate_step, gates + 4)
                    dve.reciprocal(meta[:, bass.ds(G.n * Q, Q), 2], total_exp[:]).then_inc(s2_place, 1)

                def split_weights(G):
                    if isinstance(G.n, int) and G.n >= GROUPS - 4:
                        quarter = E * KC // 4
                        c = slice((G.n - GROUPS + 4) * quarter, (G.n - GROUPS + 5) * quarter)
                        dve.wait_ge(s2_wd, 1)
                        dve.scalar_tensor_tensor(Wd_lo[:, c, :], Wd_sb[:, c, :], W_SCALE, Wd_hi[:, c, :],
                                                 ALU.mult, ALU.subtract)
                        if G.n == GROUPS - 4:
                            dve.scalar_tensor_tensor(bd2[LO:LO + 1], bd_sb[LO:LO + 1], W_SCALE, bd2[LO:LO + 1],
                                                     ALU.mult, ALU.subtract)

                dve.wait_ge(s2_const, 8)
                run_stages(dve,
                           Phase(GROUPS, 2, START1, [
                    (2, V_out), (2, C_heads((0,))), (0, stats_of), (3, divide(0)), (2, C_heads((1,))),
                    (1, e_out), (3, divide(1)), (3, invert), (2, C_heads((2,))), (0, normalise), (4, add_elu),
                    (2, C_heads((3,)))]),
                           Phase(GROUPS, 2, START2, [
                    (5, places), (1, normalise2), (4, choose), (4, one_hot), (0, stats_of2), (1, low_part),
                    (4, sum_up), (4, split_weights)]))

                steps = [0]

                def step(instruction):
                    steps[0] += 1
                    instruction.then_inc(s3, 1)
                    dve.wait_ge(s3, steps[0])

                dve.wait_ge(s2_total, 1)
                step(dve.tensor_copy(count[:], total_ps[0:1, 0:E]))
                step(dve.tensor_tensor(tail_f[:], count[:], base_e[0:1, :], ALU.add))
                dve.tensor_copy(tail_i[:], tail_f[:]).then_inc(s3_tail, 1)
                step(dve.tensor_scalar(count_i[:], count[:], float(P - 1), None, ALU.add))
                step(dve.tensor_scalar(blocks_i[:], count_i[:], P.bit_length() - 1, None, ALU.arith_shift_right))
                step(dve.tensor_scalar(blocks_f[:], blocks_i[:], float(P), None, ALU.mult))
                step(dve.tensor_scalar(room[:], blocks_f[0:1, :], -1.0, float(LIST), ALU.mult, ALU.add))
                step(dve.tensor_copy(cum[0][:], blocks_f[:]))
                n = 0
                for shift in (1, 2, 4):
                    dve.tensor_copy(cum[1 - n][:, 0:shift], cum[n][:, 0:shift])
                    step(dve.tensor_tensor(cum[1 - n][:, shift:], cum[n][:, shift:], cum[n][:, 0:E - shift], ALU.add))
                    n = 1 - n
                dve.wait_ge(s3_const, 1)
                step(dve.tensor_tensor(past[:], cum[n][0:1, :].unsqueeze(1).broadcast_to([1, SLOTS, E]),
                                       slot_f[:].unsqueeze(2).broadcast_to([1, SLOTS, E]), ALU.is_le))
                dve.tensor_reduce(expert_f[:], past[:], AX.X, ALU.add)
                step(dve.tensor_tensor(jumps[:], past[:], room[:].unsqueeze(1).broadcast_to([1, SLOTS, E]), ALU.mult))
                step(dve.tensor_reduce(start_f[:], jumps[:], AX.X, ALU.add))
                step(dve.tensor_tensor(start_f[:], start_f[:], slot_f[:], ALU.add))
                step(dve.tensor_scalar(start_i[:], start_f[:], float(E * LIST), None, ALU.min))
                dve.tensor_scalar(expert_i[:], expert_f[:], float(E - 1), float(KC), ALU.min, ALU.mult)

        phases123.close()

        NB4 = 3
        H_sb = [sb(f"p4_H{i}", [P, KC, GT]) for i in range(NB4)]
        xT_hi = [sb(f"p4_xT_hi{i}", [P, GT], F16) for i in range(NB4)]
        xT_lo = [sb(f"p4_xT_lo{i}", [P, GT], F16) for i in range(NB4)]
        idx_out = [sb(f"idx_out{i}", [P, Q], U32) for i in range(NB4)]
        xg = [sb(f"xg{i}", [P, Q, ROW]) for i in range(NB4)]
        xn4 = [sb(f"xn4_{i}", [P, Q, F]) for i in range(NB4)]
        H_hi = [sb(f"H_hi{i}", [P, KC, GT], F16) for i in range(NB4)]
        H_lo = [sb(f"H_lo{i}", [P, KC, GT], F16) for i in range(NB4)]
        yo = [sb(f"yo{i}", [P, Q, F]) for i in range(NB4)]
        y_ps = bank[5:8]
        s4_in = [[sem(f"p4_rows_loaded{i}_{q}") for q in range(Q)] for i in range(NB4)]
        s4_xn = sem("p4_normalised")
        s4_xT = sem("p4_transposed")
        s4_hi = sem("p4_high_part")
        s4_lo = sem("p4_low_part")
        s4_h = sem("p4_hidden_chunks")
        s4_gelu = sem("p4_gelu_chunks")
        s4_Hhi = sem("p4_H_high_chunks")
        s4_Hlo = sem("p4_H_low_chunks")
        s4_Hlo_pool = sem("p4_H_last_low_chunk")
        s4_y = sem("p4_expert_tiles")
        s4_yo = sem("p4_rows_ready")
        s4_out = [sem(f"p4_rows_stored{i}") for i in range(NB4)]
        START4 = 6

        def values_of(eng, table, G, largest):
            return nc.values_load_multi_w_load_instructions(
                table[0:1, bass.ds(G.n * Q, Q)], engines=[eng.engine], min_val=0, max_val=largest)[1]

        with nc.Block() as block:
            @block.sync
            def _(sp):
                def load(G):
                    starts = values_of(sp, start_i, G, E * LIST)
                    for q in range(Q):
                        if from_group(G, 3):
                            sp.wait_ge(s4_yo, Q * (G.n - 3) + q + 1)
                        sp.dma_start(xg[G.p][:, q, :], lists[bass.ds(starts[q], P), :]).then_inc(s4_in[G.p][q], 16)

                run_stages(sp, Phase(SGROUPS, NB4, START4, [(0, load)]))

            @block.gpsimd
            def _(pool):
                def H_low(G):
                    wait_apart(pool, s4_Hhi, KC * G.n + 1, s_passed)
                    if from_group(G, 3):
                        wait_apart(pool, s4_y, Q * (G.n - 2), s_passed)
                    pool.tensor_tensor(H_lo[G.p][:, 0, :], H_sb[G.p][:, 0, :], H_hi[G.p][:, 0, :],
                                       ALU.subtract).then_inc(s4_Hlo_pool, 1)

                def scatter(G):
                    wait_apart(pool, s4_yo, Q * (G.n + 1), s_passed)
                    for q in range(Q):
                        pool.indirect_dma_start(
                            out=out[:, :], out_offset=bass.IndirectOffsetOnAxis(ap=idx_out[G.p][:, q:q + 1], axis=0),
                            in_=yo[G.p][:, q, :], in_offset=None, bounds_check=B * N - 1, oob_is_err=False
                        ).then_inc(s4_out[G.p], 16)

                run_stages(pool, Phase(SGROUPS, NB4, START4, [(2, H_low), (3, scatter)]))
                for i in range(NB4):
                    pool.wait_ge(s4_out[i], 16 * Q * SGROUPS // NB4)

            @block.scalar
            def _(act):
                def high_part(G):
                    act.wait_ge(s4_xT, G.n + 1)
                    if from_group(G, 3):
                        act.wait_ge(s4_h, KC * (G.n - 2))
                    act.activation(xT_hi[G.p][:], xT_ps[:], ACT.Copy).then_inc(s4_hi, 1)

                def gelu(k):
                    def body(G):
                        if k == 0 and from_group(G, 3):
                            act.wait_ge(s4_y, Q * (G.n - 2))
                        act.wait_ge(s4_h, KC * G.n + k + 1)
                        act.activation(H_sb[G.p][:, k, :], h_ps[k][:], ACT.Gelu, bias=b1_sb[:, k:k + 1],
                                       scale=1.0 / W_SCALE).then_inc(s4_gelu, 1)
                    return body

                def H_high(k):
                    def body(G):
                        act.wait_ge(s4_gelu, KC * G.n + k + 1)
                        act.activation(H_hi[G.p][:, k, :], H_sb[G.p][:, k, :], ACT.Copy).then_inc(s4_Hhi, 1)
                    return body

                run_stages(act, Phase(SGROUPS, NB4, START4, [
                    (2, gelu(0)), (2, gelu(1)), (2, H_high(0)), (2, H_high(1)), (2, gelu(2)), (1, high_part),
                    (2, H_high(2)), (2, gelu(3)), (2, H_high(3))]))

            @block.tensor
            def _(pe):
                def transposes(G):
                    pe.wait_ge(s4_xn, G.n + 1)
                    if from_group(G, 1):
                        pe.wait_ge(s4_lo, G.n)
                    for q in range(Q):
                        last = pe.transpose(xT_ps[:, q * P:(q + 1) * P], xn4[G.p][:, q, :], ident[:])
                    last.then_inc(s4_xT, 1)

                def hidden(k, part):
                    W_part, x_part = ((W1_hi, xT_lo), (W1_lo, xT_hi), (W1_hi, xT_hi))[part]

                    def body(G):
                        if k == 0 and part == 0:
                            pe.wait_ge(s4_lo, G.n + 1)
                        if part == 0 and from_group(G, 1):
                            pe.wait_ge(s4_gelu, KC * (G.n - 1) + k + 1)
                        last = pe.matmul(h_ps[k][:], W_part[:, k * P:(k + 1) * P], x_part[G.p][:],
                                         start=(part == 0), stop=(part == 2))
                        if part == 2:
                            last.then_inc(s4_h, 1)
                    return body

                chosen = [None] * Q

                def load_experts(G):
                    chosen[:] = values_of(pe, expert_i, G, (E - 1) * KC)

                def expert(q, k):
                    def body(G):
                        if q == 0 and k == 0:
                            pe.wait_ge(s4_Hlo, 3 * (G.n + 1))
                            pe.wait_ge(s4_Hlo_pool, G.n + 1)
                        y = y_ps[(G.p + q) % NB4][:, 0:F]
                        if k == 0 and (from_group(G, 1) or q >= NB4):
                            pe.wait_ge(s4_yo, Q * G.n + q + 1 - NB4)
                        tile = (slice(None), k, slice(q * P, (q + 1) * P))
                        W_low = Wd_lo[:, bass.ds(chosen[q], KC), :][:, k, :]
                        W_high = Wd_hi[:, bass.ds(chosen[q], KC), :][:, k, :]
                        pe.matmul(y, H_hi[G.p][tile], W_low, start=(k == 0), stop=False)
                        pe.matmul(y, H_hi[G.p][tile], W_high, start=False, stop=False)
                        pe.matmul(y, H_lo[G.p][tile], W_high, start=False, stop=False)
                        if k == KC - 1:
                            bias = bd2[:, bass.ds(chosen[q], KC), :].rearrange("p k c -> p (k c)")
                            pe.matmul(y, ones16[0:LO + 1, :], bias, start=False, stop=True).then_inc(s4_y, 1)
                    return body

                def two_tiles(q0, k_hidden):
                    work = [(3, expert(q0 + n // KC, n % KC)) for n in range(2 * KC)]
                    for part, n in ((2, 6), (1, 3), (0, 0)):
                        work.insert(n, (2, hidden(k_hidden, part)))
                    return work

                first = [(2, hidden(k, part)) for k in range(2) for part in range(3)]
                run_stages(pe, Phase(SGROUPS, NB4, START4,
                           first + [(3, load_experts)] + two_tiles(0, 2) + [(1, transposes)] + two_tiles(2, 3)))

            @block.vector
            def _(dve):
                def normalise(G):
                    if from_group(G, 3):
                        dve.wait_ge(s4_xT, G.n - 2)
                    for q in range(Q):
                        dve.wait_ge(s4_in[G.p][q], 16 * (G.k + 1))
                        last = dve.tensor_scalar(xn4[G.p][:, q, :], xg[G.p][:, q, 0:F], xg[G.p][:, q, F:F + 1],
                                                 xg[G.p][:, q, F + 1:F + 2], ALU.subtract, ALU.mult)
                    last.then_inc(s4_xn, 1)

                def low_part(G):
                    dve.wait_ge(s4_hi, G.n + 1)
                    dve.tensor_tensor(xT_lo[G.p][:], xT_ps[:], xT_hi[G.p][:], ALU.subtract).then_inc(s4_lo, 1)

                def H_low(k):
                    def body(G):
                        dve.wait_ge(s4_Hhi, KC * G.n + k + 1)
                        dve.tensor_tensor(H_lo[G.p][:, k, :], H_sb[G.p][:, k, :], H_hi[G.p][:, k, :], ALU.subtract
                                          ).then_inc(s4_Hlo, 1)
                    return body

                def combine(tiles):
                    def body(G):
                        if 0 in tiles:
                            if from_group(G, 3):
                                dve.wait_ge(s4_out[G.p], 16 * Q * G.k)
                            dve.tensor_copy(idx_out[G.p][:], xg[G.p][:, :, ROW - 1])
                        for q in tiles:
                            dve.wait_ge(s4_y, Q * G.n + q + 1)
                            dve.scalar_tensor_tensor(
                                yo[G.p][:, q, :], y_ps[(G.p + q) % NB4][:, 0:F],
                                xg[G.p][:, q, F + 2:F + 3], xg[G.p][:, q, 0:F], ALU.mult, ALU.add
                            ).then_inc(s4_yo, 1)
                    return body

                run_stages(dve, Phase(SGROUPS, NB4, START4, [
                    (3, H_low(3)), (1, normalise), (2, H_low(1)), (3, combine((0, 1))), (1, low_part),
                    (2, H_low(2)), (3, combine((2, 3)))]))


_INS = ["x", "adj", "L0_gnn_W", "L0_gnn_a", "L0_ffn_W1", "L0_ffn_b1", "L0_ffn_Wg", "L0_ffn_bg",
        "L0_ffn_Wd", "L0_ffn_bd"]


def kernel(**inputs):
    import numpy as np
    import concourse.bacc as bacc
    from concourse.bass_utils import run_bass_kernel_spmd

    nc = bacc.Bacc("TRN2", target_bir_lowering=False, num_devices=1)
    arrays, args = {}, []
    for name in _INS:
        v = np.ascontiguousarray(inputs[name])
        if name == "x":
            v = v.reshape(B * N, F)
        arrays[f"in_{name}"] = v
        args.append(nc.dram_tensor(f"in_{name}", v.shape, mybir.dt.from_np(v.dtype), kind="ExternalInput").ap())
    out = nc.dram_tensor("out", (B * N, F), F32, kind="ExternalOutput").ap()
    build(nc, *args, out)
    r = run_bass_kernel_spmd(nc, [arrays], core_ids=[0])
    return r.results[0]["out"].reshape(B, N, F)
```
